# Optimizing a Trainium2 kernel written in Bass

```python
import numpy as np
import jax
import jax.numpy as jnp

def _softmax(x, axis=-1):
    return jax.nn.softmax(x, axis=axis)

def _gelu(x):
    return jax.nn.gelu(x, approximate=True)

def _silu(x):
    return jax.nn.silu(x)

def _sigmoid(x):
    return jax.nn.sigmoid(x)

def _layernorm(x, axis=-1, eps=1e-05):
    m = jnp.mean(x, axis=axis, keepdims=True)
    v = jnp.var(x, axis=axis, keepdims=True)
    return (x - m) / jnp.sqrt(v + eps)

def _scatter_add(tgt, idx, src, axis=0):
    return tgt.at[idx].add(src)

def _segment_sum(src, seg, n):
    return jax.ops.segment_sum(src, seg, n)
kernel_name = 'mk_recurrent_d1_jaxref_r8_88a42d'

def setup_inputs(seed: int=0):
    np.random.seed(seed)
    _w = jnp.asarray

    def _L0_attn_setup():
        import jax, jax.numpy as jnp
        import numpy as np
        B, S, M = (1, 256, 256)
        H, HKV, D = (32, 8, 64)
        SW = 128
        WAVELENGTH = 150000.0
        SCALE = D ** (-0.25)
        NEG = -1000000000.0

        def _cos_sin(seq_len, dtype):
            half = D // 2
            inv_freq = 1.0 / WAVELENGTH ** (jnp.arange(half, dtype=jnp.float32) * 2.0 / D)
            t = jnp.arange(seq_len, dtype=jnp.float32)
            freqs = t[:, None] * inv_freq[None, :]
            return (jnp.cos(freqs)[None, :, None, :].astype(dtype), jnp.sin(freqs)[None, :, None, :].astype(dtype))

        def _interleaved_rope(x, cos, sin):
            x_even = x[..., ::2]
            x_odd = x[..., 1::2]
            first = x_even * cos - x_odd * sin
            second = x_odd * cos + x_even * sin
            return jnp.stack([first, second], axis=-1).reshape(x.shape)
        key = jax.random.key(seed)
        ks = jax.random.split(key, 8)
        return {'hidden_states': jax.random.normal(ks[0], (B, S, M), jnp.float32), 'Wq': jax.random.normal(ks[1], (M, H, D), jnp.float32) * 0.02, 'bq': jnp.zeros((H, D), jnp.float32), 'Wk': jax.random.normal(ks[2], (M, HKV, D), jnp.float32) * 0.02, 'bk': jnp.zeros((HKV, D), jnp.float32), 'Wv': jax.random.normal(ks[3], (M, HKV, D), jnp.float32) * 0.02, 'bv': jnp.zeros((HKV, D), jnp.float32), 'Wo': jax.random.normal(ks[4], (H, D, M), jnp.float32) * 0.02, 'bo': jnp.zeros((M,), jnp.float32), 'sinks': jax.random.normal(ks[5], (H,), jnp.float32)}
    _L0_attn_in = _L0_attn_setup()

    def _L0_ffn_setup():
        import jax, jax.numpy as jnp
        import numpy as np
        FP8_MAX = 448.0
        SCALE_EPS = 1e-07
        key = jax.random.key(seed)
        k1, k2, k3 = jax.random.split(key, 3)
        in_f, out_f = (256, 256)
        x = jax.random.normal(k1, (4, 512, in_f), dtype=jnp.float32)
        w_fp32 = jax.random.normal(k2, (out_f, in_f), dtype=jnp.float32) * (1.0 / np.sqrt(in_f))
        weight = w_fp32.astype(jnp.float8_e4m3fn).astype(jnp.float32)
        weight_scale = jnp.ones((), dtype=jnp.float32)
        bound = 1.0 / np.sqrt(in_f)
        bias = jax.random.uniform(k3, (out_f,), dtype=jnp.float32, minval=-bound, maxval=bound)
        return {'x': x, 'weight': weight, 'weight_scale': weight_scale, 'bias': bias}
    _L0_ffn_in = _L0_ffn_setup()
    _d = {'L0_attn_hidden_states': _L0_attn_in['hidden_states'], 'L0_attn_Wq': _L0_attn_in['Wq'], 'L0_attn_bq': _L0_attn_in['bq'], 'L0_attn_Wk': _L0_attn_in['Wk'], 'L0_attn_bk': _L0_attn_in['bk'], 'L0_attn_Wv': _L0_attn_in['Wv'], 'L0_attn_bv': _L0_attn_in['bv'], 'L0_attn_Wo': _L0_attn_in['Wo'], 'L0_attn_bo': _L0_attn_in['bo'], 'L0_attn_sinks': _L0_attn_in['sinks'], 'L0_ffn_weight': _L0_ffn_in['weight'], 'L0_ffn_weight_scale': _L0_ffn_in['weight_scale'], 'L0_ffn_bias': _L0_ffn_in['bias']}
    _x0 = _d['L0_attn_hidden_states']
    _d['L0_attn_hidden_states'] = jax.random.normal(jax.random.fold_in(jax.random.key(seed), 1), (8, 512, 256), dtype=_x0.dtype)
    del _x0
    return _d

def reference(L0_attn_hidden_states, L0_attn_Wq, L0_attn_bq, L0_attn_Wk, L0_attn_bk, L0_attn_Wv, L0_attn_bv, L0_attn_Wo, L0_attn_bo, L0_attn_sinks, L0_ffn_weight, L0_ffn_weight_scale, L0_ffn_bias):

    def _L0_attn_ref(hidden_states, Wq, bq, Wk, bk, Wv, bv, Wo, bo, sinks):
        import jax, jax.numpy as jnp
        import numpy as np
        B, S, M = (1, 256, 256)
        H, HKV, D = (32, 8, 64)
        SW = 128
        WAVELENGTH = 150000.0
        SCALE = D ** (-0.25)
        NEG = -1000000000.0

        def _cos_sin(seq_len, dtype):
            half = D // 2
            inv_freq = 1.0 / WAVELENGTH ** (jnp.arange(half, dtype=jnp.float32) * 2.0 / D)
            t = jnp.arange(seq_len, dtype=jnp.float32)
            freqs = t[:, None] * inv_freq[None, :]
            return (jnp.cos(freqs)[None, :, None, :].astype(dtype), jnp.sin(freqs)[None, :, None, :].astype(dtype))

        def _interleaved_rope(x, cos, sin):
            x_even = x[..., ::2]
            x_odd = x[..., 1::2]
            first = x_even * cos - x_odd * sin
            second = x_odd * cos + x_even * sin
            return jnp.stack([first, second], axis=-1).reshape(x.shape)
        b, s, _ = hidden_states.shape
        groups = H // HKV
        q = jnp.einsum('bqm,muh->bquh', hidden_states, Wq) + bq
        k = jnp.einsum('bkm,mvh->bkvh', hidden_states, Wk) + bk
        v = jnp.einsum('bkm,mvh->bkvh', hidden_states, Wv) + bv
        cos, sin = _cos_sin(s, hidden_states.dtype)
        q = _interleaved_rope(q, cos, sin) * SCALE
        k = _interleaved_rope(k, cos, sin) * SCALE
        k = jnp.repeat(k, groups, axis=2)
        v = jnp.repeat(v, groups, axis=2)
        scores = jnp.einsum('bquh,bkuh->buqk', q, k)
        pos = jnp.arange(s)
        sw_mask = jnp.abs(pos[:, None] - pos[None, :]) <= SW
        scores = jnp.where(sw_mask[None, None, :, :], scores, NEG)
        sink_logits = jnp.broadcast_to(sinks[None, :, None, None], (b, H, s, 1))
        combined = jnp.concatenate([scores, sink_logits], axis=-1)
        probs = jax.nn.softmax(combined.astype(jnp.float32), axis=-1)
        attn = probs[..., :-1].astype(hidden_states.dtype)
        out = jnp.einsum('buqk,bkuh->bquh', attn, v)
        return jnp.einsum('bquh,uhm->bqm', out, Wo) + bo

    def _L0_ffn_ref(x, weight, weight_scale, bias):
        import jax, jax.numpy as jnp
        import numpy as np
        FP8_MAX = 448.0
        SCALE_EPS = 1e-07
        scale = jnp.maximum(jnp.max(jnp.abs(x)) / FP8_MAX, SCALE_EPS)
        x_q = (x / scale).astype(jnp.float8_e4m3fn).astype(jnp.float32)
        w = weight * weight_scale
        out = jnp.einsum('bsi,oi->bso', x_q, w) + bias
        return out
    x = L0_attn_hidden_states
    xn = _layernorm(x, axis=-1)
    s = _L0_attn_ref(xn, L0_attn_Wq, L0_attn_bq, L0_attn_Wk, L0_attn_bk, L0_attn_Wv, L0_attn_bv, L0_attn_Wo, L0_attn_bo, L0_attn_sinks)
    g = _silu(_L0_ffn_ref(xn, L0_ffn_weight, L0_ffn_weight_scale, L0_ffn_bias))
    x = x + s * g
    return x

_drawn_inputs = setup_inputs


def setup_inputs(seed=0):
    import zlib

    import numpy as np

    out = dict(_drawn_inputs(seed))
    spreads = {'L0_attn_bq': (0.0, 0.8),
     'L0_attn_bk': (0.0, 0.8),
     'L0_attn_bv': (0.0, 0.1),
     'L0_attn_bo': (0.0, 0.1)}
    factors = {'L0_attn_Wq': 2.981, 'L0_attn_Wk': 2.863, 'L0_attn_sinks': 8.0, 'L0_ffn_bias': 64.0}
    for name, (base, spread) in spreads.items():
        noise = np.random.default_rng([zlib.crc32(name.encode()), seed]).standard_normal(out[name].shape)
        drawn = base * np.exp(spread * noise) if base else spread * noise
        out[name] = jnp.asarray(drawn.astype(out[name].dtype))
    for name, factor in factors.items():
        out[name] = (out[name] * factor).astype(out[name].dtype)
    return out
```

```python
from contextlib import ExitStack

import numpy as np
import concourse.bass as bass
import concourse.mybir as mybir

F32 = mybir.dt.float32
F32R = mybir.dt.float32r
BF16 = mybir.dt.bfloat16
U32 = mybir.dt.uint32
ALU = mybir.AluOpType
ACT = mybir.ActivationFunctionType
AX = mybir.AxisListType

P = 128
BATCH, SEQ, M = 8, 512, 256
HEADS, KV, D = 32, 8, 64
GROUP = HEADS // KV
TILES = SEQ // P
KT = M // P
QW = GROUP * D
ROT = QW + D
PW = ROT + D
HW = 2 * D + 2
QKW = GROUP * HW + 3 * D
DV = D + 1
WINDOW = 128
WAVELENGTH = 150000.0
SCALE = D ** -0.25
LN_EPS = 1e-5
FP8_MAX, SCALE_EPS = 448.0, 1e-7
MASKED = -1e30
LOWEST = -3e38
EXPONENT_BITS = 0x7F800000
FP8_MIN_NORMAL = 2.0 ** -6
ROUND_TO_4_BITS = 1.5 * 2.0 ** 20
NP = 5
SIGMOID_LOWEST = -87.0
CHUNK = 1536
W_CHUNKS, O_CHUNKS = 2 * KT, 4
N_CHUNKS = W_CHUNKS + O_CHUNKS + 1

BLOCKS = [[k for k in (t - 1, t + 1, t) if 0 <= k < TILES] for t in range(TILES)]
FIRST = [sum(len(b) for b in BLOCKS[:t]) for t in range(TILES + 1)]
CUT = [sum(len(b) - 1 for b in BLOCKS[:t]) for t in range(TILES + 1)]
NB, NCUT = FIRST[-1], CUT[-1]



def at(eng, sem, per, step, k):
    if isinstance(step, int) and per * step + k <= 0:
        return
    eng.wait_ge(sem, step * per + k)


def stand_apart(eng, passed):
    eng.sem_inc(passed, 1)


def run_steps(eng, step, start, turn, end):
    step(-2, 0, 0, None, None, True)
    step(-1, 1, 1, 0, None, False)
    with eng.Fori(0, BATCH) as b:
        start(b)
        with eng.Fori(0, KV // 2 - 1) as p:
            step(b * KV + p * 2, 0, p * 2 + 2, p * 2 + 1, p * 2, False)
            step(b * KV + p * 2 + 1, 1, p * 2 + 3, p * 2 + 2, p * 2 + 1, False)
        turn(b)
        step(b * KV + (KV - 2), 0, 0, KV - 1, KV - 2, True)
        step(b * KV + (KV - 1), 1, 1, 0, KV - 1, False)
        end(b)


def gated_window_attention(nc, x, w_qkv, b_qkv, w_o, b_o, sinks, w_ffn, w_scale, b_ffn, rope_cos, rope_sin, out):
    x_t = x.rearrange("b (t p) m -> b p t m", p=P)
    out_t = out.rearrange("b (t p) m -> b p t m", p=P)

    with ExitStack() as ctx:
        def sb(name, shape, dt):
            return ctx.enter_context(nc.sbuf_tensor(name, shape, dt))

        w_hi = sb("w_hi", [P, KT, KV * PW], F32R)
        w_lo = sb("w_lo", [P, KT, KV * PW], F32R)
        wo_hi = sb("wo_hi", [P, KV * KT * M], F32R)
        wo_lo = sb("wo_lo", [P, KV * KT * M], F32R)
        ffn_hi = sb("ffn_hi", [P, KT * M], F32R)
        ffn_lo = sb("ffn_lo", [P, KT * M], F32R)
        bias = sb("bias", [P, KV * PW], F32)
        ffn_bias = sb("ffn_bias", [P, M], F32)
        bo_row = sb("bo_row", [1, 2 * M], F32)
        cos = sb("cos", [P, TILES, D], F32)
        sin = sb("sin", [P, TILES, D], F32)
        neg_sink = sb("neg_sink", [P, HEADS], F32)
        scale_w = sb("scale_w", [P, 1], F32)
        ident = sb("ident", [P, P], F32)
        ident_r = sb("ident_r", [P, P], F32R)
        ones = sb("ones", [1, P], F32)
        mask = sb("mask", [P, 3 * P], F32)
        eps = sb("eps", [P, TILES], F32)
        minus_half = sb("minus_half", [P, TILES], F32)
        x_in = sb("x_in", [P, TILES, M], F32)
        x_res = sb("x_res", [P, TILES, M], F32)
        xn = sb("xn", [P, TILES, M], F32)
        xq = sb("xq", [P, TILES, M], F32R)
        xT_hi = sb("xT_hi", [P, KT, SEQ], F32R)
        xT_lo = sb("xT_lo", [P, KT, SEQ], F32R)
        xqT = sb("xqT", [P, KT, SEQ], F32R)
        gate = sb("gate", [P, TILES, M], F32)
        ffn_e = sb("ffn_e", [P, 2, M], F32)
        stats = sb("stats", [P, TILES, 6], F32)
        moments = sb("moments", [P, TILES, 2], F32)
        var_eps = sb("var_eps", [P, TILES], F32)
        rstd = sb("rstd", [P, TILES], F32)
        absmax = sb("absmax", [P, BATCH], F32)
        amax = sb("amax", [P, 1], F32)
        scale_row = sb("scale_row", [1, 4], F32)
        inv_scale = sb("inv_scale", [P, 1], F32)
        proj = sb("proj", [P, 2, PW], F32)
        turn_c = sb("turn_c", [P, ROT], F32)
        turn_s = sb("turn_s", [P, ROT], F32)
        turned = sb("turned", [P, 2, ROT], F32)
        qk_parts = sb("qk_parts", [P, TILES, QKW], F32R)
        v_new = sb("v_new", [P, TILES, D], F32)
        v = sb("v", [P, 2, TILES, DV], F32)
        qT_full = sb("qT_full", [P, TILES, GROUP * P], F32R)
        qT_high = sb("qT_high", [P, TILES, GROUP * P], F32R)
        kT_high = sb("kT_high", [P, 2, SEQ], F32R)
        kT_low = sb("kT_low", [P, 2, SEQ], F32R)
        junk = sb("junk", [P, GROUP, 3 * P], BF16)
        row_max = sb("row_max", [P, GROUP], F32)
        neg_max = sb("neg_max", [P, GROUP], F32)
        sink_arg = sb("sink_arg", [P, TILES, GROUP], F32)
        sink_exp = sb("sink_exp", [P, 2, TILES, GROUP], F32)
        stage = sb("stage", [P, 2 * CHUNK], F32)
        prob = stage[:, 0:NP * GROUP * P].rearrange("p (s n) -> p s n", s=NP)
        den = sb("den", [P, GROUP], F32)
        rden = sb("rden", [P, GROUP], F32)
        o_norm = sb("o_norm", [P, GROUP, D], F32)
        oT_hi = sb("oT_hi", [P, 2, KT * P], F32R)
        oT_lo = sb("oT_lo", [P, 2, KT * P], F32R)

        def bank(name):
            return ctx.enter_context(nc.psum_tensor(name, [P, 512], F32))

        ring = [bank(f"ring{i}") for i in range(3)]
        score = [bank(f"score{i}") for i in range(2)]
        pv_bank = bank("pv_bank")
        acc = [bank(f"acc{i}") for i in range(2)]
        pv = pv_bank[:, 0:GROUP * DV].rearrange("p (h d) -> p h d", h=GROUP)

        def sem(name):
            return ctx.enter_context(nc.semaphore(name))

        s_const_in = sem("const_in")
        s_id_memset = sem("id_memset")
        s_id_ready = sem("id_ready")
        s_ones_ready = sem("ones_ready")
        s_w_hi_done = sem("w_hi_done")
        s_w_lo_done = sem("w_lo_done")
        s_w_scaled = sem("w_scaled")
        s_x_got = sem("x_got")
        s_res_got = sem("res_got")
        s_out_put = sem("out_put")
        s_ln_bn = sem("ln_bn")
        s_ln_stat = sem("ln_stat")
        s_ln_eps = sem("ln_eps")
        s_ln_rstd = sem("ln_rstd")
        s_xn_done = sem("xn_done")
        s_ln_done = sem("ln_done")
        s_amax_done = sem("amax_done")
        s_amax_pe = sem("amax_pe")
        s_amax_self = sem("amax_self")
        s_scale_pe = sem("scale_pe")
        s_inv_ready = sem("inv_ready")
        s_sink_negated = sem("sink_negated")
        s_quant_self = sem("quant_self")
        s_xq_done = sem("xq_done")
        s_ffn_pe = sem("ffn_pe")
        s_ffn_z = sem("ffn_z")
        s_ffn_clamped = sem("ffn_clamped")
        s_ffn_exp = sem("ffn_exp")
        s_ffn_self = sem("ffn_self")
        s_gate_done = sem("gate_done")
        s_xT_pe = sem("xT_pe")
        s_xT_hi_done = sem("xT_hi_done")
        s_xT_lo_done = sem("xT_lo_done")
        s_xqT_pe = sem("xqT_pe")
        s_xqT_done = sem("xqT_done")
        s_fin_read = sem("fin_read")
        s_fin_done = sem("fin_done")
        s_proj_pe = sem("proj_pe")
        s_proj_done = sem("proj_done")
        s_turn_self = sem("turn_self")
        s_turned_done = sem("turned_done")
        s_hi_done = sem("hi_done")
        s_lo_done = sem("lo_done")
        s_v_new_done = sem("v_new_done")
        s_v_ready = sem("v_ready")
        s_qfull_pe = sem("qfull_pe")
        s_qfull_done = sem("qfull_done")
        s_kT_pe = sem("kT_pe")
        s_kT_done = sem("kT_done")
        s_qhigh_pe = sem("qhigh_pe")
        s_qhigh_done = sem("qhigh_done")
        s_max_pe = sem("max_pe")
        s_max_done = sem("max_done")
        s_small_self = sem("small_self")
        s_mh_done = sem("mh_done")
        s_neg_done = sem("neg_done")
        s_sink_done = sem("sink_done")
        s_score_pe = sem("score_pe")
        s_exp_done = sem("exp_done")
        s_cut_done = sem("cut_done")
        s_pv_pe = sem("pv_pe")
        s_norm_self = sem("norm_self")
        s_norm_done = sem("norm_done")
        s_oT_pe = sem("oT_pe")
        s_oT_hi_done = sem("oT_hi_done")
        s_oT_lo_done = sem("oT_lo_done")
        s_wo_pe = sem("wo_pe")
        s_dve_passed = sem("dve_passed")
        s_pool_passed = sem("pool_passed")
        s_sp_passed = sem("sp_passed")
        stage_in = [ctx.enter_context(nc.semaphore(f"stage_in{j}")) for j in range(2)]
        block = ctx.enter_context(nc.Block())

        consts = [(scale_w[:, :], w_scale.partition_broadcast(P)), (neg_sink[:, :], sinks.partition_broadcast(P)),
                  (cos[:, :, :], rope_cos), (sin[:, :, :], rope_sin), (ffn_bias[:, :], b_ffn.partition_broadcast(P)),
                  (bo_row[0:1, 0:M], b_o.rearrange("(a m) -> a m", a=1)),
                  (bo_row[0:1, M:2 * M], b_o.rearrange("(a m) -> a m", a=1)),
                  (bias[:, :], b_qkv.partition_broadcast(P))]

        half = KV * PW // 2
        chunks = [(w_qkv[k, :, j * half:(j + 1) * half], w_hi[:, k, j * half:(j + 1) * half],
                   w_lo[:, k, j * half:(j + 1) * half]) for k in range(KT) for j in range(2)]
        chunks.append((w_ffn, ffn_hi[:, :], ffn_lo[:, :]))
        wide = KV * KT * M // O_CHUNKS
        chunks += [(w_o[:, j * wide:(j + 1) * wide], wo_hi[:, j * wide:(j + 1) * wide],
                    wo_lo[:, j * wide:(j + 1) * wide]) for j in range(O_CHUNKS)]
        FFN_CHUNK = W_CHUNKS

        def staged(n):
            width = chunks[n][1].shape[-1]
            return stage[:, (n % 2) * CHUNK:(n % 2) * CHUNK + width]

        @block.sync
        def _(sp):
            for n in range(max(BATCH, N_CHUNKS)):
                if n < BATCH:
                    if n >= 2:
                        sp.wait_ge(s_ln_done, n - 1)
                    buf, got = (x_in, s_x_got) if n % 2 == 0 else (x_res, s_res_got)
                    sp.dma_start(buf[:, :, :], x_t[n]).then_inc(got, 16)
                if n >= 2:
                    sp.wait_ge(s_w_lo_done, n - 1)
                sp.dma_start(staged(n), chunks[n][0]).then_inc(stage_in[n % 2], 16)
                if n == 1:
                    for dst, src in consts:
                        sp.dma_start(dst, src).then_inc(s_const_in, 16)
            sp.wait_ge(s_ln_done, BATCH)
            sp.dma_start(x_in[:, :, :], x_t[0]).then_inc(s_x_got, 16)

            def batch(b, this, following):
                sp.wait_ge(s_xq_done, b * 2 + 2)
                sp.dma_start(x_in[:, :, :], following).then_inc(s_x_got, 16)
                sp.dma_start(x_res[:, :, :], this).then_inc(s_res_got, 16)
                sp.wait_ge(s_fin_done, b * 2 + 2)
                return b

            with sp.Fori(0, BATCH - 1) as b:
                batch(b, x_t[bass.ds(b, 1)][0], x_t[bass.ds(b + 1, 1)][0])
                sp.dma_start(out_t[bass.ds(b, 1)][0], x_res[:, :, :]).then_inc(s_out_put, 16)
                sp.wait_ge(s_out_put, b * 16 + 16)
                stand_apart(sp, s_sp_passed)
            batch(BATCH - 1, x_t[BATCH - 1], x_t[0])
            sp.dma_start(out_t[BATCH - 1], x_res[:, :, :]).then_inc(s_out_put, 16)
            sp.wait_ge(s_x_got, 16 * (BATCH // 2 + BATCH + 1))
            sp.wait_ge(s_out_put, 16 * BATCH)

        @block.gpsimd
        def _(pool):
            nc.gpsimd.memset(ident[:, :], 0.0).then_inc(s_id_memset, 1)
            nc.gpsimd.memset(mask[:, :], 0.0).then_inc(s_id_memset, 1)
            nc.gpsimd.memset(eps[:, :], LN_EPS).then_inc(s_id_memset, 1)
            nc.gpsimd.memset(minus_half[:, :], -0.5).then_inc(s_id_memset, 1)
            nc.gpsimd.memset(v[:, :, :, :], 1.0).then_inc(s_id_memset, 1)
            nc.gpsimd.memset(ones[:, :], 1.0).then_inc(s_ones_ready, 1)
            pool.wait_ge(s_id_memset, 5)
            nc.gpsimd.affine_select(out=ident[:, :], in_=ident[:, :], compare_op=ALU.not_equal, fill=1.0, base=0,
                                    pattern=[[-1, P]], channel_multiplier=1).then_inc(s_id_ready, 1)
            nc.gpsimd.affine_select(out=mask[:, 0:P], in_=mask[:, 0:P], compare_op=ALU.is_ge, fill=MASKED, base=0,
                                    pattern=[[1, P]], channel_multiplier=-1).then_inc(s_id_ready, 1)
            nc.gpsimd.affine_select(out=mask[:, 2 * P:], in_=mask[:, 2 * P:], compare_op=ALU.is_ge, fill=MASKED,
                                    base=0, pattern=[[-1, P]], channel_multiplier=1).then_inc(s_id_ready, 1)

            def rstd_of(n):
                pool.wait_ge(s_ln_stat, n + 1)
                nc.gpsimd.tensor_tensor(var_eps[:, :], moments[:, :, 1], eps[:, :], ALU.add).then_inc(s_ln_eps, 1)
                pool.wait_ge(s_ln_eps, n + 1)
                nc.gpsimd.tensor_tensor(rstd[:, :], var_eps[:, :], minus_half[:, :], ALU.pow).then_inc(s_ln_rstd, 1)

            def keep_v(b, par):
                at(pool, s_v_new_done, TILES, b, TILES)
                stand_apart(pool, s_pool_passed)
                nc.gpsimd.tensor_copy(v[:, par, :, 0:D], v_new[:, :, :]).then_inc(s_v_ready, 1)

            def turn(a, q, par):
                slot = q % 2
                at(pool, s_proj_done, TILES, a, q + 1)
                if q == 0 and par is not None:
                    keep_v(a - 1, par)
                at(pool, s_turned_done, TILES, a, q)
                x_qk = proj[:, slot, 0:ROT]
                cos_q = cos[:, q, :].rearrange("p (a d) -> p a d", a=1).broadcast_to([P, GROUP + 1, D])
                sin_q = sin[:, q, :].rearrange("p (a i t) -> p a i t", a=1, t=2) \
                    .broadcast_to([P, GROUP + 1, D // 2, 2])
                nc.gpsimd.tensor_tensor(turn_c[:, :].rearrange("p (h d) -> p h d", d=D),
                                        x_qk.rearrange("p (h d) -> p h d", d=D), cos_q, ALU.mult) \
                    .then_inc(s_turn_self, 1)
                nc.gpsimd.tensor_tensor(turn_s[:, :].rearrange("p (h i t) -> p h i t", i=D // 2, t=2),
                                        x_qk.rearrange("p (h i t) -> p h i t", i=D // 2, t=2)[:, :, :, ::-1],
                                        sin_q, ALU.mult).then_inc(s_turn_self, 1)
                at(pool, s_v_ready, 1, a, 0)
                stand_apart(pool, s_pool_passed)
                nc.gpsimd.tensor_copy(v_new[:, q, :], proj[:, slot, ROT:PW]).then_inc(s_v_new_done, 1)
                at(pool, s_turn_self, 2 * TILES, a, 2 * q + 2)
                at(pool, s_hi_done, 2 * TILES, a, 2 * q - 2)
                at(pool, s_lo_done, TILES, a, q - 1)
                nc.gpsimd.tensor_tensor(turned[:, slot, :], turn_c[:, :], turn_s[:, :], ALU.add) \
                    .then_inc(s_turned_done, 1)

            def cut(c, q):
                for n, k in enumerate(BLOCKS[q]):
                    if k == q:
                        continue
                    blk = FIRST[q] + n
                    at(pool, s_exp_done, NB, c, blk + 1)
                    sign = 1 if k > q else -1
                    pr = prob[:, blk % NP, :].rearrange("p (h n) -> p h n", h=GROUP)
                    stand_apart(pool, s_pool_passed)
                    nc.gpsimd.affine_select(out=pr, in_=pr, compare_op=ALU.is_ge, fill=0.0, base=0,
                                            pattern=[[0, GROUP], [sign, P]], channel_multiplier=-sign) \
                        .then_inc(s_cut_done, 1)

            def step(it, even, a, b, c, fresh):
                for q in range(TILES):
                    if c is not None:
                        cut(it, q)
                    turn(it + 2, q, 1 - even if b is not None else None)

            for n in range(BATCH + 1):
                rstd_of(n)
            run_steps(pool, step, start=lambda b: rstd_of(b + (BATCH + 1)), turn=lambda b: None, end=lambda b: None)

        @block.scalar
        def _(act):
            for n, (_, hi, _) in enumerate(chunks):
                act.wait_ge(stage_in[n % 2], 16 * (n // 2 + 1))
                if n == FFN_CHUNK:
                    act.wait_ge(s_const_in, 16 * len(consts))
                    nc.scalar.activation(staged(n), staged(n), ACT.Copy, scale=scale_w[:, 0:1]).then_inc(s_w_scaled, 1)
                    act.wait_ge(s_w_scaled, 1)
                nc.scalar.activation(hi, staged(n), ACT.Copy).then_inc(s_w_hi_done, 1)
            act.wait_ge(s_id_ready, 1)
            nc.scalar.activation(ident_r[:, :], ident[:, :], ACT.Copy).then_inc(s_id_ready, 1)

            def x_turned(n):
                at(act, s_proj_pe, TILES * KV, n, 0)
                for k in range(KT):
                    act.wait_ge(s_xT_pe, n * KT + (k + 1))
                    nc.scalar.activation(xT_hi[:, k, :], ring[(2 + k) % 3][:, :], ACT.Copy).then_inc(s_xT_hi_done, 1)
                for k in range(KT):
                    act.wait_ge(s_xqT_pe, n * KT + (k + 1))
                    nc.scalar.activation(xqT[:, k, :], ring[(1 + k) % 3][:, :], ACT.Copy).then_inc(s_xqT_done, 1)

            def ffn_exp(b, j):
                act.wait_ge(s_ffn_clamped, b * 2 + (j + 1))
                nc.scalar.activation(ffn_e[:, :, :], ffn_e[:, :, :], ACT.Exp, scale=-1.0) \
                    .then_inc(s_ffn_exp, 1)

            def next_batch(b):
                ffn_exp(b, 0)
                x_turned(b + 1)
                ffn_exp(b, 1)

            def exps(c, q, n):
                blk = FIRST[q] + n
                at(act, s_score_pe, NB, c, blk + 1)
                if blk >= NP:
                    before = max(t for t in range(TILES) if FIRST[t] <= blk - NP)
                    at(act, s_pv_pe, TILES, c, before + 1)
                nc.scalar.activation(prob[:, blk % NP, :], score[blk % 2][:, :], ACT.Exp).then_inc(s_exp_done, 1)

            def q_full(b, q):
                at(act, s_qfull_pe, TILES, b, q + 1)
                nc.scalar.activation(qT_full[:, q, :], ring[0][:, :], ACT.Copy).then_inc(s_qfull_done, 1)

            def k_turned(b, par):
                at(act, s_kT_pe, 2, b, 1)
                nc.scalar.activation(kT_high[:, par, :], ring[2][:, :], ACT.Copy).then_inc(s_kT_done, 1)
                at(act, s_kT_pe, 2, b, 2)
                nc.scalar.activation(kT_low[0:D, par, :], ring[2][0:D, :], ACT.Copy).then_inc(s_kT_done, 1)

            def q_high(b, q):
                at(act, s_qhigh_pe, TILES, b, q + 1)
                nc.scalar.activation(qT_high[0:D + 2, q, :], ring[0][0:D + 2, :], ACT.Copy).then_inc(s_qhigh_done, 1)

            def sink_term(b, q, par):
                at(act, s_neg_done, TILES, b, q + 1)
                nc.scalar.activation(sink_exp[:, par, q, :], sink_arg[:, q, :], ACT.Exp).then_inc(s_sink_done, 1)

            def split_hi(a, q):
                at(act, s_turned_done, TILES, a, q + 1)
                at(act, s_qhigh_pe, TILES, a - 1, q + 1)
                if q == 0:
                    at(act, s_kT_pe, 2, a - 1, 2)
                parts = qk_parts[:, q, 0:(GROUP + 1) * HW].rearrange("p (h w) -> p h w", w=HW)
                nc.scalar.activation(parts[:, :, D:2 * D], turned[:, q % 2, :].rearrange("p (h d) -> p h d", d=D),
                                     ACT.Copy).then_inc(s_hi_done, 1)
                nc.scalar.activation(qk_parts[:, q, QKW - D:QKW], turned[:, q % 2, QW:ROT], ACT.Copy) \
                    .then_inc(s_hi_done, 1)

            def o_high(c, q):
                at(act, s_oT_pe, TILES, c, q + 1)
                nc.scalar.activation(oT_hi[:, q % 2, :], ring[2][:, 0:KT * P], ACT.Copy).then_inc(s_oT_hi_done, 1)

            def step(it, even, a, b, c, fresh):
                for q in range(TILES):
                    if c is not None:
                        exps(it, q, 0)
                        exps(it, q, 1)
                    if c is not None and q > 0:
                        o_high(it, q - 1)
                    if c is not None and len(BLOCKS[q]) > 2:
                        exps(it, q, 2)
                    if b is not None:
                        q_full(it + 1, q)
                        if q == 0:
                            k_turned(it + 1, 1 - even)
                    if b is not None:
                        sink_term(it + 1, q, 1 - even)
                        q_high(it + 1, q)
                    split_hi(it + 2, q)
                    if c is not None and q == TILES - 1:
                        o_high(it, q)

            x_turned(0)
            run_steps(act, step, start=lambda b: None, turn=next_batch, end=lambda b: None)

        @block.vector
        def _(dve):
            def normalise(n, buf):
                at(dve, s_xn_done, 1, n, 0)
                for t in range(TILES):
                    nc.vector.bn_stats(stats[:, t, :], buf[:, t, :]).then_inc(s_ln_bn, 1)
                for t in range(TILES):
                    at(dve, s_ln_bn, TILES, n, t + 1)
                    stand_apart(dve, s_dve_passed)
                    last = nc.vector.bn_aggr(moments[:, t, :], stats[:, t, :])
                last.then_inc(s_ln_stat, 1)
                at(dve, s_ln_rstd, 1, n, 1)
                for t in range(TILES):
                    last = nc.vector.tensor_scalar(xn[:, t, :], buf[:, t, :], moments[:, t, 0:1], rstd[:, t:t + 1],
                                                   ALU.subtract, ALU.mult)
                last.then_inc(s_xn_done, 1)

            nc.vector.memset(kT_low[D:D + 32, :, :].bitcast(F32), 1.0).then_inc(s_ones_ready, 1)
            for n in range(max(BATCH, N_CHUNKS)):
                if n < BATCH:
                    if n:
                        dve.wait_ge(s_ln_done, n)
                    dve.wait_ge(s_x_got if n % 2 == 0 else s_res_got, 16 * (n // 2 + 1))
                    normalise(n, x_in if n % 2 == 0 else x_res)
                    dve.wait_ge(s_xn_done, n + 1)
                    nc.vector.tensor_reduce(absmax[:, n:n + 1], xn[:, :, :], AX.XY, ALU.max,
                                            apply_absolute_value=True).then_inc(s_ln_done, 1)
                _, hi, lo = chunks[n]
                dve.wait_ge(s_w_hi_done, n + 1)
                nc.vector.tensor_tensor(lo, staged(n), hi.bitcast(F32), ALU.subtract).then_inc(s_w_lo_done, 1)
            dve.wait_ge(s_ln_done, BATCH)
            nc.vector.tensor_reduce(amax[:, :], absmax[:, :], AX.X, ALU.max).then_inc(s_amax_done, 1)
            dve.wait_ge(s_amax_pe, 1)
            nc.vector.tensor_reduce(scale_row[:, 0:1], ring[0][0:1, 0:P], AX.X, ALU.max).then_inc(s_amax_self, 1)
            dve.wait_ge(s_amax_self, 1)
            nc.vector.tensor_scalar(scale_row[:, 1:2], scale_row[:, 0:1], 1.0 / FP8_MAX, SCALE_EPS, ALU.mult, ALU.max) \
                .then_inc(s_amax_self, 1)
            dve.wait_ge(s_amax_self, 2)
            nc.vector.reciprocal(scale_row[:, 2:3], scale_row[:, 1:2]).then_inc(s_amax_self, 1)
            dve.wait_ge(s_scale_pe, 1)
            nc.vector.tensor_copy(inv_scale[:, :], ring[1][:, 0:1]).then_inc(s_inv_ready, 1)
            dve.wait_ge(s_const_in, 16 * len(consts))
            nc.vector.tensor_scalar(neg_sink[:, :], neg_sink[:, :], -1.0, None, ALU.mult).then_inc(s_sink_negated, 1)
            dve.wait_ge(s_inv_ready, 1)
            dve.wait_ge(s_sink_negated, 1)

            def quantise(n):
                at(dve, s_xn_done, 1, n, BATCH + 1)
                at(dve, s_xqT_pe, KT, n, 0)
                nc.vector.tensor_scalar(x_in[:, :, :], xn[:, :, :], inv_scale[:, 0:1], None, ALU.mult) \
                    .then_inc(s_quant_self, 1)
                for j in range(2):
                    val, big = x_in[:, 2 * j:2 * j + 2, :], ffn_e[:, :, :]
                    at(dve, s_quant_self, 7, n, 3 * j + 1)
                    if j:
                        at(dve, s_xq_done, 2, n, 1)
                    nc.vector.tensor_scalar(big.bitcast(U32), val.bitcast(U32), EXPONENT_BITS, None,
                                            ALU.bitwise_and).then_inc(s_quant_self, 1)
                    at(dve, s_quant_self, 7, n, 3 * j + 2)
                    nc.vector.tensor_scalar(big, big, FP8_MIN_NORMAL, ROUND_TO_4_BITS, ALU.max, ALU.mult) \
                        .then_inc(s_quant_self, 1)
                    at(dve, s_quant_self, 7, n, 3 * j + 3)
                    nc.vector.tensor_tensor(val, val, big, ALU.add).then_inc(s_quant_self, 1)
                    at(dve, s_quant_self, 7, n, 3 * j + 4)
                    nc.vector.tensor_tensor(xq[:, 2 * j:2 * j + 2, :], val, big, ALU.subtract).then_inc(s_xq_done, 1)

            def prepare(n):
                at(dve, s_x_got, 16, n, 16 * (BATCH // 2 + 1))
                at(dve, s_xT_pe, KT, n, 0)
                normalise(n + BATCH, x_in)
                quantise(n)

            def x_low(n):
                at(dve, s_proj_pe, TILES * KV, n, 0)
                for k in range(KT):
                    at(dve, s_xT_hi_done, KT, n, k + 1)
                    nc.vector.tensor_tensor(xT_lo[:, k, :], ring[(2 + k) % 3][:, :], xT_hi[:, k, :].bitcast(F32),
                                            ALU.subtract).then_inc(s_xT_lo_done, 1)

            def next_batch(b):
                for j in range(2):
                    dve.wait_ge(s_ffn_pe, b * 2 + (j + 1))
                    nc.vector.tensor_tensor(gate[:, 2 * j:2 * j + 2, :],
                                            ring[j][:, :].rearrange("p (t m) -> p t m", t=2),
                                            ffn_bias[:, :].rearrange("p (a m) -> p a m", a=1)
                                            .broadcast_to([P, 2, M]), ALU.add).then_inc(s_ffn_z, 1)
                for j in range(2):
                    if j:
                        dve.wait_ge(s_gate_done, b * 2 + 1)
                    dve.wait_ge(s_ffn_z, b * 2 + (j + 1))
                    nc.vector.tensor_scalar(ffn_e[:, :, :], gate[:, 2 * j:2 * j + 2, :], SIGMOID_LOWEST, None,
                                            ALU.max).then_inc(s_ffn_clamped, 1)
                    if j == 0:
                        x_low(b + 1)
                    dve.wait_ge(s_ffn_exp, b * 2 + (j + 1))
                    nc.vector.tensor_scalar(ffn_e[:, :, :], ffn_e[:, :, :], 1.0, None, ALU.add).then_inc(s_ffn_self, 1)
                    dve.wait_ge(s_ffn_self, b * 4 + (2 * j + 1))
                    nc.vector.reciprocal(ffn_e[:, :, :], ffn_e[:, :, :]).then_inc(s_ffn_self, 1)
                    dve.wait_ge(s_ffn_self, b * 4 + (2 * j + 2))
                    nc.vector.tensor_tensor(gate[:, 2 * j:2 * j + 2, :], gate[:, 2 * j:2 * j + 2, :], ffn_e[:, :, :],
                                            ALU.mult).then_inc(s_gate_done, 1)

            def finish(b):
                at(dve, s_res_got, 16, b, 16 * (BATCH // 2 + 1))
                dve.wait_ge(s_gate_done, b * 2 + 2)
                for j in range(2):
                    dve.wait_ge(s_wo_pe, b * (TILES * KV) + (TILES * KV - 2 + 2 * j) if j else
                                b * (TILES * KV) + (TILES * KV - 2))
                    pair = gate[:, 2 * j:2 * j + 2, :]
                    nc.vector.tensor_tensor(pair, acc[j][:, :].rearrange("p (t m) -> p t m", t=2), pair, ALU.mult) \
                        .then_inc(s_fin_read, 1)
                for j in range(2):
                    dve.wait_ge(s_fin_read, b * 2 + (j + 1))
                    pair = x_res[:, 2 * j:2 * j + 2, :]
                    nc.vector.tensor_tensor(pair, pair, gate[:, 2 * j:2 * j + 2, :], ALU.add).then_inc(s_fin_done, 1)

            def projected(a, g, q):
                at(dve, s_proj_pe, TILES, a, q + 1)
                at(dve, s_turned_done, TILES, a, q - 1)
                b_g = bias[:, g * PW:(g + 1) * PW] if isinstance(g, int) else bias[:, bass.ds(g * PW, PW)]
                nc.vector.tensor_tensor(proj[:, q % 2, :], ring[1][:, 0:PW], b_g, ALU.add).then_inc(s_proj_done, 1)

            def maximum(b, q, h):
                if h == 0:
                    at(dve, s_max_done, TILES * GROUP, b, GROUP * q)
                    at(dve, s_neg_done, TILES, b, q)
                at(dve, s_max_pe, TILES * GROUP, b, GROUP * q + h + 1)
                k0 = max(q - 1, 0)
                cols = (min(q + 1, TILES - 1) - k0 + 1) * P
                m0 = (k0 - q + 1) * P
                stand_apart(dve, s_dve_passed)
                nc.vector.tensor_tensor_reduce(junk[:, h, 0:cols], ring[h % 2][:, 0:cols], mask[:, m0:m0 + cols],
                                               1.0, LOWEST, ALU.add, ALU.max, row_max[:, h:h + 1]) \
                    .then_inc(s_max_done, 1)

            def negated(b, g, q):
                at(dve, s_max_done, TILES * GROUP, b, GROUP * (q + 1))
                at(dve, s_sink_done, TILES, b - 1, q + 1)
                n_s = neg_sink[:, g * GROUP:(g + 1) * GROUP] if isinstance(g, int) else \
                    neg_sink[:, bass.ds(g * GROUP, GROUP)]
                nc.vector.tensor_scalar(neg_max[:, :], row_max[:, :], -1.0, None, ALU.mult).then_inc(s_small_self, 1)
                at(dve, s_small_self, 2 * TILES, b, 2 * q + 1)
                nc.vector.tensor_tensor(neg_max[:, :], neg_max[:, :], n_s, ALU.min).then_inc(s_small_self, 1)
                at(dve, s_small_self, 2 * TILES, b, 2 * q + 2)
                parts = qk_parts[:, q, 0:GROUP * HW].rearrange("p (h w) -> p h w", w=HW)
                nc.vector.tensor_copy(parts[:, :, 2 * D], neg_max[:, :]).then_inc(s_mh_done, 1)
                nc.vector.tensor_tensor(sink_arg[:, q, :], neg_max[:, :], n_s, ALU.subtract)
                at(dve, s_mh_done, TILES, b, q + 1)
                nc.vector.tensor_tensor(parts[:, :, 2 * D + 1], neg_max[:, :], parts[:, :, 2 * D].bitcast(F32),
                                        ALU.subtract).then_inc(s_neg_done, 1)

            def normalised(c, q, par):
                at(dve, s_sink_done, TILES, c, q + 1)
                at(dve, s_pv_pe, TILES, c, q + 1)
                nc.vector.tensor_tensor(den[:, :], pv[:, :, D], sink_exp[:, par, q, :], ALU.add) \
                    .then_inc(s_norm_self, 1)
                at(dve, s_norm_self, 2 * TILES, c, 2 * q + 1)
                nc.vector.reciprocal(rden[:, :], den[:, :]).then_inc(s_norm_self, 1)
                at(dve, s_norm_self, 2 * TILES, c, 2 * q + 2)
                nc.vector.tensor_tensor(o_norm[:, :, :], pv[:, :, 0:D],
                                        rden[:, :].rearrange("p (h a) -> p h a", a=1).broadcast_to([P, GROUP, D]),
                                        ALU.mult).then_inc(s_norm_done, 1)

            def split_lo(a, q):
                at(dve, s_hi_done, 2 * TILES, a, 2 * q + 2)
                parts = qk_parts[:, q, 0:(GROUP + 1) * HW].rearrange("p (h w) -> p h w", w=HW)
                nc.vector.tensor_tensor(parts[:, :, 0:D], turned[:, q % 2, :].rearrange("p (h d) -> p h d", d=D),
                                        parts[:, :, D:2 * D].bitcast(F32), ALU.subtract).then_inc(s_lo_done, 1)

            def o_low(c, q):
                at(dve, s_oT_hi_done, TILES, c, q + 1)
                nc.vector.tensor_tensor(oT_lo[:, q % 2, :], ring[2][:, 0:KT * P], oT_hi[:, q % 2, :].bitcast(F32),
                                        ALU.subtract).then_inc(s_oT_lo_done, 1)

            def step(it, even, a, b, c, fresh):
                for q in range(TILES):
                    if c is not None and q > 0:
                        o_low(it, q - 1)
                    projected(it + 2, a, q)
                    if b is not None:
                        for h in range(GROUP):
                            maximum(it + 1, q, h)
                        negated(it + 1, b, q)
                    if c is not None:
                        normalised(it, q, even)
                    split_lo(it + 2, q)
                    if c is not None and q == TILES - 1:
                        o_low(it, q)

            prepare(0)
            x_low(0)
            run_steps(dve, step, start=lambda b: prepare(b + 1), turn=next_batch, end=finish)

        @block.tensor
        def _(pe):
            def start_acc(b):
                for j in range(2):
                    if b is not None:
                        pe.wait_ge(s_fin_read, b * 2 + (j + 1))
                    nc.tensor.matmul(acc[j][:, :], ones[:, :], bo_row[:, :], start=True, stop=True,
                                     skip_group_check=True)

            def x_turn(n):
                if not isinstance(n, int):
                    at(pe, s_oT_hi_done, TILES * KV, n, -2 * TILES)
                    at(pe, s_oT_lo_done, TILES * KV, n, -2 * TILES)
                pe.wait_ge(s_xn_done, n + (BATCH + 1))
                for k in range(KT):
                    if k == 1:
                        at(pe, s_ffn_z, 2, n, -1)
                    for t in range(TILES):
                        last = nc.tensor.transpose(ring[(2 + k) % 3][:, t * P:(t + 1) * P],
                                                   xn[:, t, k * P:(k + 1) * P], ident[:, :])
                    last.then_inc(s_xT_pe, 1)
                pe.wait_ge(s_xq_done, n * 2 + 2)
                for k in range(KT):
                    if k == 0:
                        at(pe, s_ffn_z, 2, n, 0)
                    else:
                        pe.wait_ge(s_xT_lo_done, n * KT + 1)
                    for t in range(TILES):
                        last = nc.tensor.matmul(ring[(1 + k) % 3][:, t * P:(t + 1) * P], xq[:, t, k * P:(k + 1) * P],
                                                ident_r[:, :], start=True, stop=True)
                    last.then_inc(s_xqT_pe, 1)

            def ffn(b):
                pe.wait_ge(s_xqT_done, b * KT + KT)
                at(pe, s_qhigh_done, TILES * KV, b, TILES * (KV - 1))
                at(pe, s_max_done, TILES * GROUP * KV, b, TILES * GROUP * (KV - 1))
                for j in range(2):
                    for t in range(2):
                        tile = 2 * j + t
                        for k in range(KT):
                            for part in (ffn_hi, ffn_lo):
                                last = nc.tensor.matmul(ring[j][:, t * M:(t + 1) * M],
                                                        xqT[:, k, tile * P:(tile + 1) * P],
                                                        part[:, k * M:(k + 1) * M], start=(k == 0 and part is ffn_hi),
                                                        stop=(k == KT - 1 and part is ffn_lo))
                    last.then_inc(s_ffn_pe, 1)

            def project(a, g, q):
                n = 0
                for k in range(KT):
                    for left, right in ((xT_hi, w_hi), (xT_hi, w_lo), (xT_lo, w_hi)):
                        w_g = right[:, k, g * PW:(g + 1) * PW] if isinstance(g, int) else \
                            right[:, k, bass.ds(g * PW, PW)]
                        last = nc.tensor.matmul(ring[1][:, 0:PW], left[:, k, q * P:(q + 1) * P], w_g,
                                                start=(n == 0), stop=(n == 3 * KT - 1))
                        n += 1
                last.then_inc(s_proj_pe, 1)

            def turn_q_full(b, q):
                at(pe, s_hi_done, 2 * TILES, b, 2 * q + 2)
                at(pe, s_lo_done, TILES, b, q + 1)
                at(pe, s_qhigh_done, TILES, b, q)
                for h in range(GROUP):
                    last = nc.tensor.matmul(ring[0][:, h * P:(h + 1) * P], qk_parts[:, q, h * HW:h * HW + 2 * D],
                                            ident_r[:, :], start=True, stop=True)
                last.then_inc(s_qfull_pe, 1)

            def turn_k(b, low):
                at(pe, s_hi_done, 2 * TILES, b, 2 * TILES)
                at(pe, s_lo_done, TILES, b, TILES)
                k0 = GROUP * HW
                if low:
                    at(pe, s_kT_done, 2, b, 1)
                for t in range(TILES):
                    src = qk_parts[:, t, k0:k0 + D] if low else qk_parts[:, t, k0 + D:k0 + 3 * D]
                    last = nc.tensor.matmul(ring[2][0:(D if low else 2 * D), t * P:(t + 1) * P], src,
                                            ident_r[:, :], start=True, stop=True)
                last.then_inc(s_kT_pe, 1)

            def turn_q_high(b, q):
                at(pe, s_neg_done, TILES, b, q + 1)
                at(pe, s_max_done, TILES * GROUP, b, GROUP * q + 3)
                for h in range(GROUP):
                    last = nc.tensor.matmul(ring[0][0:D + 2, h * P:(h + 1) * P],
                                            qk_parts[:, q, h * HW + D:h * HW + 2 * D + 2], ident_r[:, :],
                                            start=True, stop=True)
                last.then_inc(s_qhigh_pe, 1)

            def score_rows(b, q, h, par):
                if h == 0:
                    at(pe, s_qfull_done, TILES, b, q + 1)
                elif h == 1:
                    at(pe, s_proj_done, TILES, b + 1, q + 1)
                else:
                    at(pe, s_max_done, TILES * GROUP, b, GROUP * q + h - 1)
                if q == 0 and h == 0:
                    at(pe, s_kT_done, 2, b, 1)
                k0 = max(q - 1, 0)
                cols = (min(q + 1, TILES - 1) - k0 + 1) * P
                nc.tensor.matmul(ring[h % 2][:, 0:cols], qT_full[:, q, h * P:(h + 1) * P],
                                 kT_high[:, par, k0 * P:k0 * P + cols], start=True, stop=True).then_inc(s_max_pe, 1)

            def scores(c, q, n, par):
                k, blk = BLOCKS[q][n], FIRST[q] + n
                if n == 0:
                    at(pe, s_qhigh_done, TILES, c, q + 1)
                    if q == 0:
                        at(pe, s_kT_done, 2, c, 2)
                if blk >= 2:
                    at(pe, s_exp_done, NB, c, blk - 1)
                nc.tensor.matmul(score[blk % 2][:, :], kT_high[:, par, k * P:(k + 1) * P], qT_full[:, q, :],
                                 start=True, stop=False)
                nc.tensor.matmul(score[blk % 2][:, :], kT_low[0:D + 2, par, k * P:(k + 1) * P],
                                 qT_high[0:D + 2, q, :], start=False, stop=True).then_inc(s_score_pe, 1)

            def weigh(c, q, par):
                if q == 0:
                    at(pe, s_v_ready, 1, c, 1)
                at(pe, s_cut_done, NCUT, c, CUT[q + 1])
                at(pe, s_exp_done, NB, c, FIRST[q + 1])
                for h in range(GROUP):
                    for n, k in enumerate(BLOCKS[q]):
                        last = nc.tensor.matmul(pv[:, h, :], prob[:, (FIRST[q] + n) % NP, h * P:(h + 1) * P],
                                                v[:, par, k, :], start=(n == 0), stop=(n == len(BLOCKS[q]) - 1))
                last.then_inc(s_pv_pe, 1)

            def turn_o(c, q):
                at(pe, s_norm_done, TILES, c, q + 1)
                if q == 0:
                    at(pe, s_kT_done, 2, c + 1, 2)
                o_flat = o_norm[:, :, :].rearrange("p h d -> p (h d)")
                for k in range(KT):
                    last = nc.tensor.transpose(ring[2][:, k * P:(k + 1) * P], o_flat[:, k * P:(k + 1) * P],
                                               ident[:, :])
                last.then_inc(s_oT_pe, 1)

            def out_project(c, g, q):
                at(pe, s_oT_hi_done, TILES, c, q + 1)
                at(pe, s_oT_lo_done, TILES, c, q + 1)
                for k in range(KT):
                    for left, right in ((oT_hi, wo_hi), (oT_hi, wo_lo), (oT_lo, wo_hi)):
                        w_g = right[:, (g * KT + k) * M:(g * KT + k + 1) * M] if isinstance(g, int) else \
                            right[:, bass.ds(g * (KT * M) + k * M, M)]
                        last = nc.tensor.matmul(acc[q // 2][:, (q % 2) * M:(q % 2 + 1) * M],
                                                left[:, q % 2, k * P:(k + 1) * P], w_g, start=False, stop=True,
                                                skip_group_check=True)
                last.then_inc(s_wo_pe, 1)

            def step(it, even, a, b, c, fresh):
                with_b, with_c = b is not None, c is not None
                odd = 1 - even
                for q in range(TILES):
                    if with_c:
                        scores(it, q, 0, even)
                        scores(it, q, 1, even)
                        if q > 0:
                            turn_o(it, q - 1)
                    if fresh and q == 0:
                        pe.wait_ge(s_xT_lo_done, turned_batches[0])
                        pe.wait_ge(s_xqT_done, turned_batches[0])
                    if with_b and q == 0:
                        turn_q_full(it + 1, 0)
                        turn_k(it + 1, False)
                    at(pe, s_proj_done, TILES, it + 2, q)
                    if with_b:
                        at(pe, s_max_done, TILES * GROUP, it + 1, GROUP * q)
                    project(it + 2, a, q)
                    if with_b and q == 0:
                        turn_k(it + 1, True)
                    if with_c and len(BLOCKS[q]) > 2:
                        scores(it, q, 2, even)
                    if with_b and q > 0:
                        turn_q_full(it + 1, q)
                    if with_c and q > 0:
                        out_project(it, c, q - 1)
                    if with_b:
                        for h in range(GROUP):
                            score_rows(it + 1, q, h, odd)
                    if with_c:
                        weigh(it, q, even)
                        if q == TILES - 1:
                            turn_o(it, q)
                    if with_b:
                        turn_q_high(it + 1, q)
                    if with_c and q == TILES - 1:
                        out_project(it, c, q)

            turned_batches = [KT]

            def next_batch(b):
                ffn(b)
                x_turn(b + 1)
                turned_batches[0] = b * KT + 2 * KT

            pe.wait_ge(s_id_ready, 4)
            pe.wait_ge(s_ones_ready, 2)
            pe.wait_ge(s_amax_done, 1)
            nc.tensor.transpose(ring[0][0:1, 0:P], amax[:, :], ident[:, :]).then_inc(s_amax_pe, 1)
            pe.wait_ge(s_amax_self, 3)
            nc.tensor.matmul(ring[1][:, 0:1], ones[:, :], scale_row[:, 2:3], start=True, stop=True) \
                .then_inc(s_scale_pe, 1)
            pe.wait_ge(s_const_in, 16 * len(consts))
            start_acc(None)
            pe.wait_ge(s_w_lo_done, N_CHUNKS)
            pe.wait_ge(s_inv_ready, 1)
            x_turn(0)
            run_steps(pe, step, start=lambda b: None, turn=next_batch, end=start_acc)


def kernel(L0_attn_hidden_states, L0_attn_Wq, L0_attn_bq, L0_attn_Wk, L0_attn_bk, L0_attn_Wv, L0_attn_bv, L0_attn_Wo,
           L0_attn_bo, L0_attn_sinks, L0_ffn_weight, L0_ffn_weight_scale, L0_ffn_bias):
    import concourse.bacc as bacc
    from concourse.bass_utils import run_bass_kernel_spmd

    def host(a):
        return np.asarray(a)

    wq = host(L0_attn_Wq).reshape(KT, P, KV, QW)
    wk = host(L0_attn_Wk).reshape(KT, P, KV, D)
    wv = host(L0_attn_Wv).reshape(KT, P, KV, D)
    w_qkv = np.concatenate([wq, wk, wv], axis=3).reshape(KT, P, KV * PW)
    b_qkv = np.concatenate([host(L0_attn_bq).reshape(KV, QW), host(L0_attn_bk), host(L0_attn_bv)], axis=1).reshape(-1)
    w_o = host(L0_attn_Wo).reshape(KV * KT, P, M).transpose(1, 0, 2).reshape(P, KV * KT * M)
    w_ffn = host(L0_ffn_weight).T.reshape(KT, P, M).transpose(1, 0, 2).reshape(P, KT * M)

    inv_freq = np.float32(1.0) / np.float32(WAVELENGTH) ** (np.arange(D // 2, dtype=np.float32) * np.float32(2.0) / D)
    freqs = np.arange(SEQ, dtype=np.float32)[:, None] * inv_freq.astype(np.float32)[None, :]
    c, sn = np.cos(freqs) * np.float32(SCALE), np.sin(freqs) * np.float32(SCALE)
    cos = np.repeat(c, 2, axis=1).reshape(TILES, P, D).transpose(1, 0, 2)
    sin = np.stack([-sn, sn], axis=-1).reshape(TILES, P, D).transpose(1, 0, 2)

    arrays = {"x": host(L0_attn_hidden_states), "w_qkv": w_qkv, "b_qkv": b_qkv, "w_o": w_o, "b_o": host(L0_attn_bo),
              "sinks": host(L0_attn_sinks), "w_ffn": w_ffn, "w_scale": host(L0_ffn_weight_scale).reshape(1),
              "b_ffn": host(L0_ffn_bias), "rope_cos": cos.astype(np.float32), "rope_sin": sin.astype(np.float32)}
    arrays = {f"in_{n}": np.ascontiguousarray(a) for n, a in arrays.items()}
    nc = bacc.Bacc("TRN2", target_bir_lowering=False, num_devices=1)
    args = [nc.dram_tensor(n, a.shape, mybir.dt.from_np(a.dtype), kind="ExternalInput").ap()
            for n, a in arrays.items()]
    out = nc.dram_tensor("out", (BATCH, SEQ, M), F32, kind="ExternalOutput").ap()
    gated_window_attention(nc, *args, out)
    result = run_bass_kernel_spmd(nc, [arrays], core_ids=[0])
    return result.results[0]["out"]
```

```python
from contextlib import ExitStack

import numpy as np
import concourse.bass as bass
import concourse.mybir as mybir

F32 = mybir.dt.float32
F32R = mybir.dt.float32r
BF16 = mybir.dt.bfloat16
U32 = mybir.dt.uint32
ALU = mybir.AluOpType
ACT = mybir.ActivationFunctionType
AX = mybir.AxisListType

P = 128
BATCH, SEQ, M = 8, 512, 256
HEADS, KV, D = 32, 8, 64
GROUP = HEADS // KV
TILES = SEQ // P
KT = M // P
QW = GROUP * D
ROT = QW + D
PW = ROT + D
HW = 2 * D + 2
QKW = GROUP * HW + 3 * D
DV = D + 1
WINDOW = 128
WAVELENGTH = 150000.0
SCALE = D ** -0.25
LN_EPS = 1e-5
FP8_MAX, SCALE_EPS = 448.0, 1e-7
MASKED = -1e30
LOWEST = -3e38
EXPONENT_BITS = 0x7F800000
FP8_MIN_NORMAL = 2.0 ** -6
ROUND_TO_4_BITS = 1.5 * 2.0 ** 20
NP = 6
SIGMOID_LOWEST = -87.0
CHUNK = 1536
W_CHUNKS, O_CHUNKS = 2 * KT, 4
N_CHUNKS = W_CHUNKS + O_CHUNKS + 1

BLOCKS = [[k for k in (t - 1, t + 1, t) if 0 <= k < TILES] for t in range(TILES)]
FIRST = [sum(len(b) for b in BLOCKS[:t]) for t in range(TILES + 1)]
CUT = [sum(len(b) - 1 for b in BLOCKS[:t]) for t in range(TILES + 1)]
NB, NCUT = FIRST[-1], CUT[-1]



def at(eng, sem, per, step, k):
    if isinstance(step, int) and per * step + k <= 0:
        return
    eng.wait_ge(sem, step * per + k)


def stand_apart(eng, passed):
    eng.sem_inc(passed, 1)


def back(step, q, n):
    return (step, q - n) if q >= n else (step - 1, q - n + TILES)


def of_group(tensor, group, width):
    return tensor[:, group * width:(group + 1) * width] if isinstance(group, int) else \
        tensor[:, bass.ds(group * width, width)]


def run_steps(eng, step):
    step(-2, 0, (0, None, None, None))
    step(-1, 1, (1, 0, None, None))
    with eng.Fori(0, BATCH) as n:
        for k in (0, 1):
            step(n * KV + k, k, (k + 2, k + 1, k, (k - 1) % KV), n, k)
        with eng.Fori(1, KV // 2 - 1) as pair:
            for k in (0, 1):
                g = pair * 2 + k
                step(n * KV + g, k, (g + 2, g + 1, g, g - 1))
        for k in (KV - 2, KV - 1):
            step(n * KV + k, k % 2, ((k + 2) % KV, (k + 1) % KV, k, k - 1), n, k)


def gated_window_attention(nc, x, w_qkv, b_qkv, w_o, b_o, sinks, w_ffn, w_scale, b_ffn, rope_cos, rope_sin, out):
    x_t = x.rearrange("b (t p) m -> b p t m", p=P)
    out_t = out.rearrange("b (t p) m -> b p t m", p=P)

    with ExitStack() as ctx:
        def sb(name, shape, dt):
            return ctx.enter_context(nc.sbuf_tensor(name, shape, dt))

        w_hi = sb("w_hi", [P, KT, KV * PW], F32R)
        w_lo = sb("w_lo", [P, KT, KV * PW], F32R)
        wo_hi = sb("wo_hi", [P, KV * KT * M], F32R)
        wo_lo = sb("wo_lo", [P, KV * KT * M], F32R)
        ffn_hi = sb("ffn_hi", [P, KT * M], F32R)
        ffn_lo = sb("ffn_lo", [P, KT * M], F32R)
        bias = sb("bias", [P, KV * PW], F32)
        ffn_bias = sb("ffn_bias", [P, M], F32)
        bo_row = sb("bo_row", [1, 2 * M], F32)
        cos = sb("cos", [P, TILES, D], F32)
        sin = sb("sin", [P, TILES, D], F32)
        neg_sink = sb("neg_sink", [P, HEADS], F32)
        scale_w = sb("scale_w", [P, 1], F32)
        ident = sb("ident", [P, P], F32)
        ident_r = sb("ident_r", [P, P], F32R)
        ident_b = sb("ident_b", [P, P], BF16)
        ones = sb("ones", [1, P], F32)
        mask = sb("mask", [P, 3 * P], F32)
        eps = sb("eps", [P, TILES], F32)
        minus_half = sb("minus_half", [P, TILES], F32)
        x_in = sb("x_in", [P, TILES, M], F32)
        x_res = sb("x_res", [P, 2, M], F32)
        xn = sb("xn", [P, TILES, M], F32)
        xq = xn[:, :, :].bitcast(BF16)[:, :, 0:M]
        xT_hi = sb("xT_hi", [P, KT, SEQ], F32R)
        xT_lo = sb("xT_lo", [P, KT, SEQ], F32R)
        xqT = sb("xqT", [P, KT, SEQ], F32R)
        gate = sb("gate", [P, TILES, M], F32)
        ffn_e = sb("ffn_e", [P, 2, M], F32)
        stats = sb("stats", [P, TILES, 6], F32)
        moments = sb("moments", [P, TILES, 2], F32)
        var_eps = sb("var_eps", [P, TILES], F32)
        rstd = sb("rstd", [P, TILES], F32)
        absmax = sb("absmax", [P, BATCH], F32)
        amax = sb("amax", [P, 1], F32)
        scale_row = sb("scale_row", [1, 4], F32)
        inv_scale = sb("inv_scale", [P, 1], F32)
        proj = sb("proj", [P, 2, PW], F32)
        turn_s = sb("turn_s", [P, ROT], F32)
        turned = sb("turned", [P, 2, ROT], F32)
        qk_parts = sb("qk_parts", [P, 2, TILES, QKW], F32R)
        v_new = sb("v_new", [P, TILES, D], F32)
        v = sb("v", [P, 2, TILES, DV], F32)
        qT_full = sb("qT_full", [P, TILES, GROUP * P], F32R)
        qT_high = sb("qT_high", [P, TILES, GROUP * P], F32R)
        kT_high = sb("kT_high", [P, 2, SEQ], F32R)
        kT_low = sb("kT_low", [P, 2, SEQ], F32R)
        junk = sb("junk", [P, 2, 3 * P], BF16)
        row_max = sb("row_max", [P, GROUP], F32)
        neg_max = sb("neg_max", [P, GROUP], F32)
        sink_arg = sb("sink_arg", [P, TILES, GROUP], F32)
        sink_exp = sb("sink_exp", [P, 2, TILES, GROUP], F32)
        stage = sb("stage", [P, 2 * CHUNK], F32)
        prob = stage[:, 0:NP * GROUP * P].rearrange("p (s n) -> p s n", s=NP)
        den = sb("den", [P, GROUP], F32)
        rden = sb("rden", [P, GROUP], F32)
        o_norm = sb("o_norm", [P, GROUP, D], F32)
        oT_hi = sb("oT_hi", [P, 2, KT * P], F32R)
        oT_lo = sb("oT_lo", [P, 2, KT * P], F32R)

        def bank(name):
            return ctx.enter_context(nc.psum_tensor(name, [P, 512], F32))

        ring = [bank(f"ring{i}") for i in range(3)]
        score = [bank(f"score{i}") for i in range(2)]
        pv_bank = bank("pv_bank")
        acc = [bank(f"acc{i}") for i in range(2)]
        pv = pv_bank[:, 0:GROUP * DV].rearrange("p (h d) -> p h d", h=GROUP)

        def sem(name):
            return ctx.enter_context(nc.semaphore(name))

        s_const_in = sem("const_in")
        s_id_memset = sem("id_memset")
        s_id_ready = sem("id_ready")
        s_ones_ready = sem("ones_ready")
        s_w_hi_done = sem("w_hi_done")
        s_w_lo_done = sem("w_lo_done")
        s_w_scaled = sem("w_scaled")
        s_x_got = sem("x_got")
        s_x_odd_got = sem("x_odd_got")
        s_res_got = sem("res_got")
        s_out_put = sem("out_put")
        s_ln_bn = sem("ln_bn")
        s_ln_stat = sem("ln_stat")
        s_ln_eps = sem("ln_eps")
        s_ln_rstd = sem("ln_rstd")
        s_xn_done = sem("xn_done")
        s_ln_done = sem("ln_done")
        s_amax_done = sem("amax_done")
        s_amax_pe = sem("amax_pe")
        s_amax_self = sem("amax_self")
        s_scale_pe = sem("scale_pe")
        s_inv_ready = sem("inv_ready")
        s_sink_negated = sem("sink_negated")
        s_quant_self = sem("quant_self")
        s_xq_done = sem("xq_done")
        s_ffn_pe = sem("ffn_pe")
        s_ffn_z = sem("ffn_z")
        s_ffn_clamped = sem("ffn_clamped")
        s_ffn_exp = sem("ffn_exp")
        s_ffn_self = sem("ffn_self")
        s_gate_done = sem("gate_done")
        s_xT_pe = sem("xT_pe")
        s_xT_hi_done = sem("xT_hi_done")
        s_xT_lo_done = sem("xT_lo_done")
        s_xqT_pe = sem("xqT_pe")
        s_xqT_done = sem("xqT_done")
        s_fin_read = sem("fin_read")
        s_fin_done = sem("fin_done")
        s_proj_pe = sem("proj_pe")
        s_proj_done = sem("proj_done")
        s_turn_self = sem("turn_self")
        s_turned_done = sem("turned_done")
        s_hi_done = sem("hi_done")
        s_lo_done = sem("lo_done")
        s_v_new_done = sem("v_new_done")
        s_v_ready = sem("v_ready")
        s_qfull_pe = sem("qfull_pe")
        s_qfull_done = sem("qfull_done")
        s_kT_pe = sem("kT_pe")
        s_kT_done = sem("kT_done")
        s_qhigh_pe = sem("qhigh_pe")
        s_qhigh_done = sem("qhigh_done")
        s_max_pe = sem("max_pe")
        s_max_done = sem("max_done")
        s_small_self = sem("small_self")
        s_mh_done = sem("mh_done")
        s_neg_done = sem("neg_done")
        s_sink_done = sem("sink_done")
        s_score_pe = sem("score_pe")
        s_exp_done = sem("exp_done")
        s_cut_done = sem("cut_done")
        s_pv_pe = sem("pv_pe")
        s_norm_self = sem("norm_self")
        s_norm_done = sem("norm_done")
        s_oT_pe = sem("oT_pe")
        s_oT_hi_done = sem("oT_hi_done")
        s_oT_lo_done = sem("oT_lo_done")
        s_wo_pe = sem("wo_pe")
        s_dve_passed = sem("dve_passed")
        s_pool_passed = sem("pool_passed")
        s_sp_passed = sem("sp_passed")
        stage_in = [ctx.enter_context(nc.semaphore(f"stage_in{j}")) for j in range(2)]
        block = ctx.enter_context(nc.Block())

        consts = [(scale_w[:, :], w_scale.partition_broadcast(P)), (neg_sink[:, :], sinks.partition_broadcast(P)),
                  (cos[:, :, :], rope_cos), (sin[:, :, :], rope_sin), (ffn_bias[:, :], b_ffn.partition_broadcast(P)),
                  (bo_row[0:1, 0:M], b_o.rearrange("(a m) -> a m", a=1)),
                  (bo_row[0:1, M:2 * M], b_o.rearrange("(a m) -> a m", a=1)),
                  (bias[:, :], b_qkv.partition_broadcast(P))]

        half = KV * PW // 2
        chunks = [(w_qkv[k, :, j * half:(j + 1) * half], w_hi[:, k, j * half:(j + 1) * half],
                   w_lo[:, k, j * half:(j + 1) * half]) for k in range(KT) for j in range(2)]
        chunks.append((w_ffn, ffn_hi[:, :], ffn_lo[:, :]))
        wide = KV * KT * M // O_CHUNKS
        chunks += [(w_o[:, j * wide:(j + 1) * wide], wo_hi[:, j * wide:(j + 1) * wide],
                    wo_lo[:, j * wide:(j + 1) * wide]) for j in range(O_CHUNKS)]
        FFN_CHUNK = W_CHUNKS

        def staged(n):
            width = chunks[n][1].shape[-1]
            return stage[:, (n % 2) * CHUNK:(n % 2) * CHUNK + width]

        @block.sync
        def _(sp):
            for n in range(max(BATCH, N_CHUNKS)):
                if n < BATCH:
                    if n >= 2:
                        sp.wait_ge(s_ln_done, n - 1)
                    buf, got = (x_in, s_x_got) if n % 2 == 0 else (gate, s_x_odd_got)
                    sp.dma_start(buf[:, :, :], x_t[n]).then_inc(got, 16)
                if n >= 2:
                    sp.wait_ge(s_w_lo_done, n - 1)
                sp.dma_start(staged(n), chunks[n][0]).then_inc(stage_in[n % 2], 16)
                if n == 1:
                    for dst, src in consts:
                        sp.dma_start(dst, src).then_inc(s_const_in, 16)
            sp.wait_ge(s_ln_done, BATCH)
            sp.dma_start(x_in[:, :, :], x_t[0]).then_inc(s_x_got, 16)
            sp.wait_ge(s_xq_done, 2)
            sp.dma_start(x_in[:, :, :], x_t[1]).then_inc(s_x_got, 16)

            def result(n, j, x_b, out_b):
                sp.dma_start(x_res[:, :, :], x_b[:, 2 * j:2 * j + 2, :]).then_inc(s_res_got, 16)
                sp.wait_ge(s_fin_done, n * 2 + (j + 1))
                if out_b is not None:
                    sp.dma_start(out_b[:, 2 * j:2 * j + 2, :], x_res[:, :, :]).then_inc(s_out_put, 16)
                    sp.wait_ge(s_out_put, n * 32 + (16 * j - 16))
                    if not isinstance(n, int):
                        stand_apart(sp, s_sp_passed)

            result(0, 0, x_t[0], None)
            result(0, 1, x_t[0], None)
            sp.wait_ge(s_xq_done, 4)
            sp.dma_start(x_in[:, :, :], x_t[2]).then_inc(s_x_got, 16)
            with sp.Fori(1, BATCH - 2) as n:
                for j in range(2):
                    result(n, j, x_t[bass.ds(n - 1, 1)][0], out_t[bass.ds(n - 1, 1)][0])
                sp.wait_ge(s_xq_done, n * 2 + 4)
                sp.dma_start(x_in[:, :, :], x_t[bass.ds(n + 2, 1)][0]).then_inc(s_x_got, 16)
            for n in range(BATCH - 2, BATCH + 1):
                for j in range(2):
                    result(n, j, x_t[n - 1], out_t[n - 1])
                if n == BATCH - 2:
                    sp.wait_ge(s_xq_done, 2 * BATCH)
                    sp.dma_start(x_in[:, :, :], x_t[0]).then_inc(s_x_got, 16)
            sp.wait_ge(s_x_got, 16 * (BATCH // 2 + BATCH + 1))

        @block.gpsimd
        def _(pool):
            nc.gpsimd.memset(ident[:, :], 0.0).then_inc(s_id_memset, 1)
            nc.gpsimd.memset(mask[:, :], 0.0).then_inc(s_id_memset, 1)
            nc.gpsimd.memset(eps[:, :], LN_EPS).then_inc(s_id_memset, 1)
            nc.gpsimd.memset(minus_half[:, :], -0.5).then_inc(s_id_memset, 1)
            nc.gpsimd.memset(v[:, :, :, :], 1.0).then_inc(s_id_memset, 1)
            nc.gpsimd.memset(ones[:, :], 1.0).then_inc(s_ones_ready, 1)
            nc.gpsimd.memset(o_norm[:, :, :], 0.0).then_inc(s_norm_done, TILES - 1)
            nc.gpsimd.memset(sink_exp[:, :, :, :], 1.0).then_inc(s_sink_done, TILES)
            nc.gpsimd.memset(oT_hi[:, :, :].bitcast(F32), 0.0).then_inc(s_oT_hi_done, TILES - 2)
            nc.gpsimd.memset(oT_lo[:, :, :].bitcast(F32), 0.0).then_inc(s_oT_lo_done, TILES - 2)
            pool.sem_inc(s_cut_done, NCUT)
            pool.wait_ge(s_id_memset, 5)
            nc.gpsimd.affine_select(out=ident[:, :], in_=ident[:, :], compare_op=ALU.not_equal, fill=1.0, base=0,
                                    pattern=[[-1, P]], channel_multiplier=1).then_inc(s_id_ready, 1)
            nc.gpsimd.affine_select(out=mask[:, 0:P], in_=mask[:, 0:P], compare_op=ALU.is_ge, fill=MASKED, base=0,
                                    pattern=[[1, P]], channel_multiplier=-1).then_inc(s_id_ready, 1)
            nc.gpsimd.affine_select(out=mask[:, 2 * P:], in_=mask[:, 2 * P:], compare_op=ALU.is_ge, fill=MASKED,
                                    base=0, pattern=[[-1, P]], channel_multiplier=1).then_inc(s_id_ready, 1)

            def rstd_of(n):
                pool.wait_ge(s_ln_stat, n + 1)
                nc.gpsimd.tensor_tensor(var_eps[:, :], moments[:, :, 1], eps[:, :], ALU.add).then_inc(s_ln_eps, 1)
                pool.wait_ge(s_ln_eps, n + 1)
                nc.gpsimd.tensor_tensor(rstd[:, :], var_eps[:, :], minus_half[:, :], ALU.pow).then_inc(s_ln_rstd, 1)

            def turn(a, q):
                slot = q % 2
                at(pool, s_proj_done, TILES, a, q + 1)
                at(pool, s_turned_done, TILES, a, q)
                at(pool, s_lo_done, TILES, a, q - 1)
                x_qk = proj[:, slot, 0:ROT]
                cos_q = cos[:, q, :].rearrange("p (a d) -> p a d", a=1).broadcast_to([P, GROUP + 1, D])
                sin_q = sin[:, q, :].rearrange("p (a i t) -> p a i t", a=1, t=2) \
                    .broadcast_to([P, GROUP + 1, D // 2, 2])
                nc.gpsimd.tensor_tensor(turned[:, slot, :].rearrange("p (h d) -> p h d", d=D),
                                        x_qk.rearrange("p (h d) -> p h d", d=D), cos_q, ALU.mult) \
                    .then_inc(s_turn_self, 1)
                nc.gpsimd.tensor_tensor(turn_s[:, :].rearrange("p (h i t) -> p h i t", i=D // 2, t=2),
                                        x_qk.rearrange("p (h i t) -> p h i t", i=D // 2, t=2)[:, :, :, ::-1],
                                        sin_q, ALU.mult).then_inc(s_turn_self, 1)
                at(pool, s_turn_self, 2 * TILES, a, 2 * q + 2)
                nc.gpsimd.tensor_tensor(turned[:, slot, :], turned[:, slot, :], turn_s[:, :], ALU.add) \
                    .then_inc(s_turned_done, 1)

            def cut(c, q):
                for n, k in enumerate(BLOCKS[q]):
                    if k == q:
                        continue
                    at(pool, s_exp_done, NB, c + 1, FIRST[q] + n + 1)
                    sign = 1 if k > q else -1
                    pr = prob[:, q % 2 * 3 + n, :].rearrange("p (h n) -> p h n", h=GROUP)
                    stand_apart(pool, s_pool_passed)
                    nc.gpsimd.affine_select(out=pr, in_=pr, compare_op=ALU.is_ge, fill=0.0, base=0,
                                            pattern=[[0, GROUP], [sign, P]], channel_multiplier=-sign) \
                        .then_inc(s_cut_done, 1)

            def step(it, par, groups, n=None, k=None):
                for q in range(TILES):
                    if groups[2] is not None:
                        cut(it, q)
                    if (k, q) == (0, 0):
                        rstd_of(n + (BATCH + 1))
                    turn(it + 2, q)

            for n in range(BATCH + 1):
                rstd_of(n)
            run_steps(pool, step)

        @block.scalar
        def _(act):
            for n, (_, hi, _) in enumerate(chunks):
                act.wait_ge(stage_in[n % 2], 16 * (n // 2 + 1))
                if n == FFN_CHUNK:
                    act.wait_ge(s_const_in, 16 * len(consts))
                    nc.scalar.activation(staged(n), staged(n), ACT.Copy, scale=scale_w[:, 0:1]).then_inc(s_w_scaled, 1)
                    act.wait_ge(s_w_scaled, 1)
                nc.scalar.activation(hi, staged(n), ACT.Copy).then_inc(s_w_hi_done, 1)
            act.wait_ge(s_id_ready, 1)
            nc.scalar.activation(ident_b[:, :], ident[:, :], ACT.Copy).then_inc(s_id_ready, 1)
            nc.scalar.activation(ident_r[:, :], ident[:, :], ACT.Copy).then_inc(s_id_ready, 1)

            act.sem_inc(s_exp_done, NB)

            def x_high(n, k):
                act.wait_ge(s_xT_pe, n * KT + (k + 1))
                nc.scalar.activation(xT_hi[:, k, :], ring[2 - k][:, :], ACT.Copy).then_inc(s_xT_hi_done, 1)

            def xq_turned(n, k):
                act.wait_ge(s_xqT_pe, n * KT + (k + 1))
                nc.scalar.activation(xqT[:, k, :], ring[2][:, :], ACT.Copy).then_inc(s_xqT_done, 1)

            def ffn_exp(b, j):
                act.wait_ge(s_ffn_clamped, b * 2 + (j + 1))
                nc.scalar.activation(ffn_e[:, :, :], ffn_e[:, :, :], ACT.Exp, scale=-1.0) \
                    .then_inc(s_ffn_exp, 1)

            def exps(c, q, n):
                at(act, s_score_pe, NB, c, FIRST[q] + n + 1)
                nc.scalar.activation(prob[:, q % 2 * 3 + n, :], score[(FIRST[q] + n) % 2][:, :], ACT.Exp) \
                    .then_inc(s_exp_done, 1)

            def q_full(b, q):
                at(act, s_qfull_pe, TILES, b, q + 1)
                nc.scalar.activation(qT_full[:, q, :], ring[0][:, :], ACT.Copy).then_inc(s_qfull_done, 1)

            def k_turned(b, par, low):
                at(act, s_kT_pe, 2, b, 1 + low)
                if low:
                    nc.scalar.activation(kT_low[0:D, par, :], ring[2][0:D, :], ACT.Copy).then_inc(s_kT_done, 1)
                else:
                    nc.scalar.activation(kT_high[:, par, :], ring[2][:, :], ACT.Copy).then_inc(s_kT_done, 1)

            def q_high(b, q, par):
                at(act, s_qhigh_pe, TILES, b, q + 1)
                nc.scalar.activation(qT_high[0:D + 2, q, :], ring[2][0:D + 2, :], ACT.Copy).then_inc(s_qhigh_done, 1)
                nc.scalar.activation(sink_exp[:, par, q, :], sink_arg[:, q, :], ACT.Exp).then_inc(s_sink_done, 1)

            def split_hi(a, q, par):
                at(act, s_turned_done, TILES, a, q + 1)
                parts = qk_parts[:, par, q, 0:(GROUP + 1) * HW].rearrange("p (h w) -> p h w", w=HW)
                nc.scalar.activation(parts[:, :, D:2 * D], turned[:, q % 2, :].rearrange("p (h d) -> p h d", d=D),
                                     ACT.Copy).then_inc(s_hi_done, 1)
                nc.scalar.activation(qk_parts[:, par, q, QKW - D:QKW], turned[:, q % 2, QW:ROT], ACT.Copy) \
                    .then_inc(s_hi_done, 1)

            def v_aside(a, q):
                at(act, s_v_ready, 1, a, 0)
                nc.scalar.activation(v_new[:, q, :], proj[:, q % 2, ROT:PW], ACT.Copy).then_inc(s_v_new_done, 1)

            def keep_v(b, par):
                at(act, s_v_new_done, TILES, b, TILES)
                at(act, s_pv_pe, TILES, b - 1, TILES)
                nc.scalar.activation(v[:, par, :, 0:D], v_new[:, :, :], ACT.Copy).then_inc(s_v_ready, 1)

            def o_high(c, q):
                at(act, s_oT_pe, TILES, c + 1, q + 1)
                nc.scalar.activation(oT_hi[:, q % 2, :], ring[2][:, 0:KT * P], ACT.Copy).then_inc(s_oT_hi_done, 1)

            def step(it, par, groups, n=None, k=None):
                _, b, c, _ = groups
                for q in range(TILES):
                    b1 = (b if q >= 1 else c) is not None
                    b2 = (b if q >= 2 else c) is not None
                    if q >= 1 or b is not None:
                        a_step, a_tile = back(it + 2, q, 1)
                        a_par = par if q >= 1 else 1 - par
                        split_hi(a_step, a_tile, a_par)
                        if q == 1 and b is not None:
                            keep_v(it + 1, 1 - par)
                        v_aside(a_step, a_tile)
                    if c is not None:
                        exps(it, q, 0)
                        exps(it, q, 1)
                    if (k, q) == (KV - 2, 0):
                        x_high(n + 1, 0)
                        x_high(n + 1, 1)
                    if b1:
                        q_full(*back(it + 1, q, 1))
                    if b is not None and q == 1:
                        k_turned(it + 1, 1 - par, 0)
                    if c is not None and len(BLOCKS[q]) > 2:
                        exps(it, q, 2)
                    if b is not None and q == 1:
                        k_turned(it + 1, 1 - par, 1)
                    if k == KV - 1 and q >= 2:
                        xq_turned(n + 1, q - 2)
                    if b2:
                        q_high(*back(it + 1, q, 2), 1 - par if q >= 2 else par)
                    if c is not None:
                        o_high(*back(it, q, 2))
                    if (k, q) == (1, 3):
                        ffn_exp(n, 0)
                    if (k, q) == (KV - 1, 2):
                        ffn_exp(n, 1)

            for k in range(KT):
                x_high(0, k)
            for k in range(KT):
                xq_turned(0, k)
            run_steps(act, step)
            for q in range(2):
                o_high(*back(BATCH * KV, q, 2))

        @block.vector
        def _(dve):
            def moments_of(n, buf):
                at(dve, s_xn_done, 1, n, 0)
                for t in range(TILES):
                    nc.vector.bn_stats(stats[:, t, :], buf[:, t, :]).then_inc(s_ln_bn, 1)
                for t in range(TILES):
                    at(dve, s_ln_bn, TILES, n, t + 1)
                    stand_apart(dve, s_dve_passed)
                    last = nc.vector.bn_aggr(moments[:, t, :], stats[:, t, :])
                last.then_inc(s_ln_stat, 1)

            def normalise(n, buf):
                at(dve, s_ln_rstd, 1, n, 1)
                at(dve, s_xqT_pe, KT, n - (BATCH + 1), KT)
                for t in range(TILES):
                    last = nc.vector.tensor_scalar(xn[:, t, :], buf[:, t, :], moments[:, t, 0:1], rstd[:, t:t + 1],
                                                   ALU.subtract, ALU.mult)
                last.then_inc(s_xn_done, 1)

            nc.vector.memset(kT_low[D:D + 32, :, :].bitcast(F32), 1.0).then_inc(s_ones_ready, 1)
            for n in range(max(BATCH, N_CHUNKS)):
                if n < BATCH:
                    if n:
                        dve.wait_ge(s_ln_done, n)
                    dve.wait_ge(s_x_got if n % 2 == 0 else s_x_odd_got, 16 * (n // 2 + 1))
                    moments_of(n, x_in if n % 2 == 0 else gate)
                    normalise(n, x_in if n % 2 == 0 else gate)
                    dve.wait_ge(s_xn_done, n + 1)
                    nc.vector.tensor_reduce(absmax[:, n:n + 1], xn[:, :, :], AX.XY, ALU.max,
                                            apply_absolute_value=True).then_inc(s_ln_done, 1)
                _, hi, lo = chunks[n]
                dve.wait_ge(s_w_hi_done, n + 1)
                nc.vector.tensor_tensor(lo, staged(n), hi.bitcast(F32), ALU.subtract).then_inc(s_w_lo_done, 1)
            dve.wait_ge(s_ln_done, BATCH)
            nc.vector.tensor_reduce(amax[:, :], absmax[:, :], AX.X, ALU.max).then_inc(s_amax_done, 1)
            dve.wait_ge(s_amax_pe, 1)
            nc.vector.tensor_reduce(scale_row[:, 0:1], ring[0][0:1, 0:P], AX.X, ALU.max).then_inc(s_amax_self, 1)
            dve.wait_ge(s_amax_self, 1)
            nc.vector.tensor_scalar(scale_row[:, 1:2], scale_row[:, 0:1], 1.0 / FP8_MAX, SCALE_EPS, ALU.mult, ALU.max) \
                .then_inc(s_amax_self, 1)
            dve.wait_ge(s_amax_self, 2)
            nc.vector.reciprocal(scale_row[:, 2:3], scale_row[:, 1:2]).then_inc(s_amax_self, 1)
            dve.wait_ge(s_scale_pe, 1)
            nc.vector.tensor_copy(inv_scale[:, :], ring[1][:, 0:1]).then_inc(s_inv_ready, 1)
            dve.wait_ge(s_const_in, 16 * len(consts))
            nc.vector.tensor_scalar(neg_sink[:, :], neg_sink[:, :], -1.0, None, ALU.mult).then_inc(s_sink_negated, 1)
            dve.wait_ge(s_inv_ready, 1)
            dve.wait_ge(s_sink_negated, 1)

            def scale_x(n):
                at(dve, s_xn_done, 1, n, BATCH + 1)
                nc.vector.tensor_scalar(x_in[:, :, :], xn[:, :, :], inv_scale[:, 0:1], None, ALU.mult) \
                    .then_inc(s_quant_self, 1)

            def quantise(n, j):
                val, big = x_in[:, 2 * j:2 * j + 2, :], ffn_e[:, :, :]
                at(dve, s_quant_self, 7, n, 3 * j + 1)
                if j:
                    at(dve, s_xq_done, 2, n, 1)
                nc.vector.tensor_scalar(big.bitcast(U32), val.bitcast(U32), EXPONENT_BITS, None,
                                        ALU.bitwise_and).then_inc(s_quant_self, 1)
                at(dve, s_quant_self, 7, n, 3 * j + 2)
                nc.vector.tensor_scalar(big, big, FP8_MIN_NORMAL, ROUND_TO_4_BITS, ALU.max, ALU.mult) \
                    .then_inc(s_quant_self, 1)
                at(dve, s_quant_self, 7, n, 3 * j + 3)
                nc.vector.tensor_tensor(val, val, big, ALU.add).then_inc(s_quant_self, 1)
                at(dve, s_quant_self, 7, n, 3 * j + 4)
                nc.vector.tensor_tensor(xq[:, 2 * j:2 * j + 2, :], val, big, ALU.subtract).then_inc(s_xq_done, 1)

            def measure(n):
                at(dve, s_x_got, 16, n, 16 * (BATCH // 2 + 1))
                moments_of(n + BATCH, x_in)

            def x_low(n, k):
                at(dve, s_xT_hi_done, KT, n, k + 1)
                nc.vector.tensor_tensor(xT_lo[:, k, :], ring[2 - k][:, :], xT_hi[:, k, :].bitcast(F32),
                                        ALU.subtract).then_inc(s_xT_lo_done, 1)

            def ffn_bias_on(b, j):
                dve.wait_ge(s_ffn_pe, b * 2 + (j + 1))
                nc.vector.tensor_tensor(gate[:, 2 * j:2 * j + 2, :],
                                        ring[2][:, :].rearrange("p (t m) -> p t m", t=2),
                                        ffn_bias[:, :].rearrange("p (a m) -> p a m", a=1)
                                        .broadcast_to([P, 2, M]), ALU.add).then_inc(s_ffn_z, 1)

            def ffn_clamp(b, j):
                dve.wait_ge(s_ffn_z, b * 2 + (j + 1))
                nc.vector.tensor_scalar(ffn_e[:, :, :], gate[:, 2 * j:2 * j + 2, :], SIGMOID_LOWEST, None,
                                        ALU.max).then_inc(s_ffn_clamped, 1)

            def ffn_gate(b, j):
                dve.wait_ge(s_ffn_exp, b * 2 + (j + 1))
                nc.vector.tensor_scalar(ffn_e[:, :, :], ffn_e[:, :, :], 1.0, None, ALU.add).then_inc(s_ffn_self, 1)
                dve.wait_ge(s_ffn_self, b * 4 + (2 * j + 1))
                nc.vector.reciprocal(ffn_e[:, :, :], ffn_e[:, :, :]).then_inc(s_ffn_self, 1)
                dve.wait_ge(s_ffn_self, b * 4 + (2 * j + 2))
                nc.vector.tensor_tensor(gate[:, 2 * j:2 * j + 2, :], gate[:, 2 * j:2 * j + 2, :], ffn_e[:, :, :],
                                        ALU.mult).then_inc(s_gate_done, 1)

            def finish(n, j):
                if j == 0:
                    dve.wait_ge(s_gate_done, n * 2 + 2)
                dve.wait_ge(s_wo_pe, n * (TILES * KV) + (2 + 2 * j))
                pair = gate[:, 2 * j:2 * j + 2, :]
                nc.vector.tensor_tensor(pair, acc[j][:, :].rearrange("p (t m) -> p t m", t=2), pair, ALU.mult) \
                    .then_inc(s_fin_read, 1)
                dve.wait_ge(s_fin_read, n * 2 + (j + 1))
                dve.wait_ge(s_res_got, n * 32 + (16 * j + 16))
                nc.vector.tensor_tensor(x_res[:, :, :], x_res[:, :, :], pair, ALU.add).then_inc(s_fin_done, 1)

            def projected(a, g, q):
                at(dve, s_proj_pe, TILES, a, q + 1)
                at(dve, s_turned_done, TILES, a, q - 1)
                at(dve, s_v_new_done, TILES, a, q - 1)
                nc.vector.tensor_tensor(proj[:, q % 2, :], ring[1][:, 0:PW], of_group(bias, g, PW), ALU.add) \
                    .then_inc(s_proj_done, 1)

            def maximum(b, q, h):
                if h == 0:
                    at(dve, s_neg_done, TILES, b, q)
                at(dve, s_max_pe, TILES * GROUP, b, GROUP * q + h + 1)
                k0 = max(q - 1, 0)
                cols = (min(q + 1, TILES - 1) - k0 + 1) * P
                m0 = (k0 - q + 1) * P
                stand_apart(dve, s_dve_passed)
                nc.vector.tensor_tensor_reduce(junk[:, h % 2, 0:cols], ring[h % 2][:, 0:cols], mask[:, m0:m0 + cols],
                                               1.0, LOWEST, ALU.add, ALU.max, row_max[:, h:h + 1]) \
                    .then_inc(s_max_done, 1)

            def negated(b, g, q, par):
                at(dve, s_max_done, TILES * GROUP, b, GROUP * (q + 1))
                at(dve, s_sink_done, TILES, b, q + 1)
                n_s = of_group(neg_sink, g, GROUP)
                nc.vector.tensor_scalar(neg_max[:, :], row_max[:, :], -1.0, None, ALU.mult).then_inc(s_small_self, 1)
                at(dve, s_small_self, 2 * TILES, b, 2 * q + 1)
                nc.vector.tensor_tensor(neg_max[:, :], neg_max[:, :], n_s, ALU.min).then_inc(s_small_self, 1)
                at(dve, s_small_self, 2 * TILES, b, 2 * q + 2)
                parts = qk_parts[:, par, q, 0:GROUP * HW].rearrange("p (h w) -> p h w", w=HW)
                nc.vector.tensor_copy(parts[:, :, 2 * D], neg_max[:, :]).then_inc(s_mh_done, 1)
                nc.vector.tensor_tensor(sink_arg[:, q, :], neg_max[:, :], n_s, ALU.subtract)
                at(dve, s_mh_done, TILES, b, q + 1)
                nc.vector.tensor_tensor(parts[:, :, 2 * D + 1], neg_max[:, :], parts[:, :, 2 * D].bitcast(F32),
                                        ALU.subtract).then_inc(s_neg_done, 1)

            def normalised(c, q, par):
                at(dve, s_sink_done, TILES, c + 1, q + 1)
                at(dve, s_pv_pe, TILES, c + 1, q + 1)
                nc.vector.tensor_tensor(den[:, :], pv[:, :, D], sink_exp[:, par, q, :], ALU.add) \
                    .then_inc(s_norm_self, 1)
                at(dve, s_norm_self, 2 * TILES, c + 1, 2 * q + 1)
                nc.vector.reciprocal(rden[:, :], den[:, :]).then_inc(s_norm_self, 1)
                at(dve, s_norm_self, 2 * TILES, c + 1, 2 * q + 2)
                nc.vector.tensor_tensor(o_norm[:, :, :], pv[:, :, 0:D],
                                        rden[:, :].rearrange("p (h a) -> p h a", a=1).broadcast_to([P, GROUP, D]),
                                        ALU.mult).then_inc(s_norm_done, 1)

            def split_lo(a, q, par):
                at(dve, s_hi_done, 2 * TILES, a, 2 * q + 2)
                parts = qk_parts[:, par, q, 0:(GROUP + 1) * HW].rearrange("p (h w) -> p h w", w=HW)
                nc.vector.tensor_tensor(parts[:, :, 0:D], turned[:, q % 2, :].rearrange("p (h d) -> p h d", d=D),
                                        parts[:, :, D:2 * D].bitcast(F32), ALU.subtract).then_inc(s_lo_done, 1)

            def o_low(c, q):
                at(dve, s_oT_hi_done, TILES, c + 1, q + 1)
                nc.vector.tensor_tensor(oT_lo[:, q % 2, :], ring[2][:, 0:KT * P], oT_hi[:, q % 2, :].bitcast(F32),
                                        ALU.subtract).then_inc(s_oT_lo_done, 1)

            def beside(n, k, q):
                if (k, q) == (0, 0):
                    measure(n + 1)
                elif (k, q) == (0, 1):
                    finish(n, 0)
                elif (k, q) == (0, 2):
                    normalise(n + (BATCH + 1), x_in)
                elif (k, q) == (0, 3):
                    finish(n, 1)
                elif (k, q) == (1, 2):
                    ffn_bias_on(n, 0)
                elif (k, q) == (1, 3):
                    ffn_bias_on(n, 1)
                    ffn_clamp(n, 0)
                elif (k, q) == (KV - 2, 0):
                    x_low(n + 1, 0)
                    x_low(n + 1, 1)
                elif (k, q) == (KV - 2, 1):
                    ffn_gate(n, 0)
                elif (k, q) == (KV - 2, 2):
                    scale_x(n + 1)
                elif (k, q) == (KV - 2, 3):
                    quantise(n + 1, 0)
                elif (k, q) == (KV - 1, 0):
                    quantise(n + 1, 1)
                elif (k, q) == (KV - 1, 2):
                    ffn_clamp(n, 1)
                elif (k, q) == (KV - 1, 3):
                    ffn_gate(n, 1)

            def step(it, par, groups, n=None, k=None):
                a, b, c, _ = groups
                for q in range(TILES):
                    b_group = b if q >= 1 else c
                    if q >= 1 or b is not None:
                        split_lo(*back(it + 2, q, 1), par if q >= 1 else 1 - par)
                    if n is not None:
                        beside(n, k, q)
                    projected(it + 2, a, q)
                    b_step, b_tile = back(it + 1, q, 1)
                    if b_group is not None:
                        for h in range(GROUP):
                            maximum(b_step, b_tile, h)
                    if c is not None:
                        o_low(*back(it, q, 2))
                    if b_group is not None:
                        negated(b_step, b_group, b_tile, 1 - par if q >= 1 else par)
                    if c is not None:
                        normalised(*back(it, q, 1), par if q >= 1 else 1 - par)

            dve.sem_inc(s_norm_self, 2 * (TILES - 1))
            dve.sem_inc(s_gate_done, 2)
            measure(0)
            normalise(BATCH, x_in)
            scale_x(0)
            x_low(0, 0)
            x_low(0, 1)
            quantise(0, 0)
            quantise(0, 1)
            run_steps(dve, step)
            o_low(*back(BATCH * KV, 0, 2))
            normalised(BATCH * KV - 1, TILES - 1, (BATCH * KV - 1) % 2)
            finish(BATCH, 0)
            o_low(*back(BATCH * KV, 1, 2))
            finish(BATCH, 1)

        @block.tensor
        def _(pe):
            def start_acc(n, j):
                if n is not None:
                    pe.wait_ge(s_fin_read, n * 2 + (j + 1))
                nc.tensor.matmul(acc[j][:, :], ones[:, :], bo_row[:, :], start=True, stop=True,
                                 skip_group_check=True)

            def ring2_read(it, q):
                at(pe, s_oT_lo_done, TILES, it + 1, q - 2)

            def turn_x(n, k):
                for t in range(TILES):
                    last = nc.tensor.transpose(ring[2 - k][:, t * P:(t + 1) * P], xn[:, t, k * P:(k + 1) * P],
                                               ident[:, :])
                last.then_inc(s_xT_pe, 1)

            def turn_xq(n, k):
                for t in range(TILES):
                    last = nc.tensor.matmul(ring[2][:, t * P:(t + 1) * P], xq[:, t, k * P:(k + 1) * P],
                                            ident_b[:, :], start=True, stop=True)
                last.then_inc(s_xqT_pe, 1)

            def ffn(b, j):
                pe.wait_ge(s_xqT_done, b * KT + KT)
                for t in range(2):
                    tile = 2 * j + t
                    for k in range(KT):
                        for part in (ffn_hi, ffn_lo):
                            last = nc.tensor.matmul(ring[2][:, t * M:(t + 1) * M], xqT[:, k, tile * P:(tile + 1) * P],
                                                    part[:, k * M:(k + 1) * M], start=(k == 0 and part is ffn_hi),
                                                    stop=(k == KT - 1 and part is ffn_lo))
                last.then_inc(s_ffn_pe, 1)

            def project(a, g, q):
                products = [(left, right, k) for k in range(KT)
                            for left, right in ((xT_hi, w_hi), (xT_hi, w_lo), (xT_lo, w_hi))]
                for n, (left, right, k) in enumerate(products):
                    last = nc.tensor.matmul(ring[1][:, 0:PW], left[:, k, q * P:(q + 1) * P],
                                            of_group(right[:, k, :], g, PW), start=(n == 0),
                                            stop=(n == len(products) - 1))
                last.then_inc(s_proj_pe, 1)

            def turn_q_full(b, q, par):
                at(pe, s_lo_done, TILES, b, q + 1)
                at(pe, s_max_done, TILES * GROUP, b, GROUP * q - 1)
                for h in range(GROUP):
                    last = nc.tensor.matmul(ring[0][:, h * P:(h + 1) * P], qk_parts[:, par, q, h * HW:h * HW + 2 * D],
                                            ident_r[:, :], start=True, stop=True)
                last.then_inc(s_qfull_pe, 1)

            def turn_k(b, par, low):
                at(pe, s_lo_done, TILES, b, TILES)
                k0 = GROUP * HW
                if low:
                    at(pe, s_kT_done, 2, b, 1)
                for t in range(TILES):
                    src = qk_parts[:, par, t, k0:k0 + D] if low else qk_parts[:, par, t, k0 + D:k0 + 3 * D]
                    last = nc.tensor.matmul(ring[2][0:(D if low else 2 * D), t * P:(t + 1) * P], src,
                                            ident_r[:, :], start=True, stop=True)
                last.then_inc(s_kT_pe, 1)

            def turn_q_high(b, q, par):
                at(pe, s_neg_done, TILES, b, q + 1)
                for h in range(GROUP):
                    last = nc.tensor.matmul(ring[2][0:D + 2, h * P:(h + 1) * P],
                                            qk_parts[:, par, q, h * HW + D:h * HW + 2 * D + 2], ident_r[:, :],
                                            start=True, stop=True)
                last.then_inc(s_qhigh_pe, 1)

            def score_rows(b, q, h, par, it, now):
                if h == 0:
                    at(pe, s_qfull_done, TILES, b, q + 1)
                elif h == 1:
                    at(pe, s_proj_done, TILES, it + 2, now + 1)
                else:
                    at(pe, s_max_done, TILES * GROUP, b, GROUP * q + h - 1)
                if q == 0 and h == 0:
                    at(pe, s_kT_done, 2, b, 1)
                k0 = max(q - 1, 0)
                cols = (min(q + 1, TILES - 1) - k0 + 1) * P
                nc.tensor.matmul(ring[h % 2][:, 0:cols], qT_full[:, q, h * P:(h + 1) * P],
                                 kT_high[:, par, k0 * P:k0 * P + cols], start=True, stop=True).then_inc(s_max_pe, 1)

            def scores(c, q, n, par):
                k, blk = BLOCKS[q][n], FIRST[q] + n
                if n == 0:
                    at(pe, s_qhigh_done, TILES, c, q + 1)
                    if q == 0:
                        at(pe, s_kT_done, 2, c, 2)
                at(pe, s_exp_done, NB, c + 1, blk - 1)
                nc.tensor.matmul(score[blk % 2][:, :], kT_high[:, par, k * P:(k + 1) * P], qT_full[:, q, :],
                                 start=True, stop=False)
                nc.tensor.matmul(score[blk % 2][:, :], kT_low[0:D + 2, par, k * P:(k + 1) * P],
                                 qT_high[0:D + 2, q, :], start=False, stop=True).then_inc(s_score_pe, 1)

            def weigh(c, q, h, par):
                if h == 0:
                    if q == 0:
                        at(pe, s_v_ready, 1, c, 1)
                    at(pe, s_exp_done, NB, c + 1, FIRST[q + 1])
                    at(pe, s_cut_done, NCUT, c + 1, CUT[q + 1])
                    at(pe, s_norm_done, TILES, c + 1, q)
                for n, k in enumerate(BLOCKS[q]):
                    last = nc.tensor.matmul(pv[:, h, :], prob[:, q % 2 * 3 + n, h * P:(h + 1) * P],
                                            v[:, par, k, :], start=(n == 0), stop=(n == len(BLOCKS[q]) - 1))
                if h == GROUP - 1:
                    last.then_inc(s_pv_pe, 1)

            def turn_o(c, q):
                at(pe, s_norm_done, TILES, c + 1, q + 1)
                o_flat = o_norm[:, :, :].rearrange("p h d -> p (h d)")
                for k in range(KT):
                    last = nc.tensor.transpose(ring[2][:, k * P:(k + 1) * P], o_flat[:, k * P:(k + 1) * P],
                                               ident[:, :])
                last.then_inc(s_oT_pe, 1)

            def out_project(c, g, q):
                at(pe, s_oT_lo_done, TILES, c + 1, q + 1)
                for k in range(KT):
                    for left, right in ((oT_hi, wo_hi), (oT_hi, wo_lo), (oT_lo, wo_hi)):
                        w_g = right[:, (g * KT + k) * M:(g * KT + k + 1) * M] if isinstance(g, int) else \
                            right[:, bass.ds(g * (KT * M) + k * M, M)]
                        last = nc.tensor.matmul(acc[q // 2][:, (q % 2) * M:(q % 2 + 1) * M],
                                                left[:, q % 2, k * P:(k + 1) * P], w_g, start=False, stop=True,
                                                skip_group_check=True)
                last.then_inc(s_wo_pe, 1)

            def beside(n, k, q):
                if (k, q) == (0, 3):
                    start_acc(n, 0)
                elif (k, q) == (1, 0):
                    start_acc(n, 1)
                elif k == 1 and q >= 2:
                    ring2_read(n * KV + k, q)
                    ffn(n, q - 2)
                elif (k, q) == (KV - 2, 0):
                    pe.wait_ge(s_xn_done, n + (BATCH + 2))
                    ring2_read(n * KV + k, q)
                    turn_x(n + 1, 0)
                    at(pe, s_max_done, TILES * GROUP, n * KV + k, TILES * GROUP - GROUP)
                    turn_x(n + 1, 1)
                elif k == KV - 1 and q >= 2:
                    pe.wait_ge(s_xq_done, n * 2 + 4)
                    ring2_read(n * KV + k, q)
                    turn_xq(n + 1, q - 2)

            def step(it, par, groups, n=None, k=None):
                a, b, c, before = groups
                with_c = c is not None
                for q in range(TILES):
                    with_b1 = (b if q >= 1 else c) is not None
                    with_b2 = (b if q >= 2 else c) is not None
                    b1, b1_par = back(it + 1, q, 1), 1 - par if q >= 1 else par
                    b2, b2_par = back(it + 1, q, 2), 1 - par if q >= 2 else par
                    c1, c1_par = back(it, q, 1), par if q >= 1 else 1 - par
                    new_x = (k, q) == (KV - 2, 0)

                    def projection():
                        if new_x:
                            pe.wait_ge(s_xT_lo_done, n * KT + 2 * KT)
                        at(pe, s_max_done, TILES * GROUP, it + 1, GROUP * (q - 1))
                        project(it + 2, a, q)

                    if with_c:
                        scores(it, q, 0, par)
                        scores(it, q, 1, par)
                    if n is not None:
                        beside(n, k, q)
                    if with_b1:
                        turn_q_full(*b1, b1_par)
                    if q == 1 and b is not None:
                        ring2_read(it, q)
                        turn_k(it + 1, 1 - par, False)
                    if not with_c:
                        at(pe, s_proj_done, TILES, it + 2, q)
                    if not new_x:
                        projection()
                    if with_c and len(BLOCKS[q]) > 2:
                        scores(it, q, 2, par)
                    if q == 1 and b is not None:
                        turn_k(it + 1, 1 - par, True)
                    if new_x:
                        pe.wait_ge(s_xT_lo_done, n * KT + (KT + 1))
                    elif k == 1 and q >= 2:
                        pe.wait_ge(s_ffn_z, n * 2 + (q - 1))
                    elif k == KV - 1 and q >= 2:
                        pe.wait_ge(s_xqT_done, n * KT + (KT + q - 1))
                    elif q == 1:
                        at(pe, s_kT_done, 2, it + 1, 2)
                    else:
                        ring2_read(it, q)
                        if not with_c or q == 0:
                            at(pe, s_qhigh_done, TILES, it + 1, q - 2)
                    if with_b2:
                        turn_q_high(*b2, b2_par)
                    for h in range(GROUP):
                        if with_b1 and h != 1:
                            score_rows(*b1, h, b1_par, it, q)
                        if new_x and h == 1:
                            projection()
                        if with_b1 and h == 1:
                            score_rows(*b1, h, b1_par, it, q)
                        if with_c:
                            weigh(*c1, h, c1_par)
                            if h == 1:
                                at(pe, s_qhigh_done, TILES, it + 1, q - 1)
                                turn_o(*back(it, q, 2))
                    if with_c:
                        out_project(*(back(it, q, 3)[0], c if q == 3 else before, back(it, q, 3)[1]))

            pe.wait_ge(s_id_ready, 5)
            pe.wait_ge(s_ones_ready, 2)
            pe.wait_ge(s_amax_done, 1)
            nc.tensor.transpose(ring[0][0:1, 0:P], amax[:, :], ident[:, :]).then_inc(s_amax_pe, 1)
            pe.wait_ge(s_amax_self, 3)
            nc.tensor.matmul(ring[1][:, 0:1], ones[:, :], scale_row[:, 2:3], start=True, stop=True) \
                .then_inc(s_scale_pe, 1)
            pe.wait_ge(s_const_in, 16 * len(consts))
            start_acc(None, 0)
            start_acc(None, 1)
            pe.wait_ge(s_w_lo_done, N_CHUNKS)
            pe.wait_ge(s_inv_ready, 1)
            pe.wait_ge(s_xn_done, BATCH + 1)
            turn_x(0, 0)
            turn_x(0, 1)
            pe.wait_ge(s_xq_done, 2)
            pe.wait_ge(s_xT_lo_done, 1)
            turn_xq(0, 0)
            pe.wait_ge(s_xqT_done, 1)
            turn_xq(0, 1)
            pe.wait_ge(s_xT_lo_done, KT)
            pe.sem_inc(s_pv_pe, TILES - 1)
            pe.sem_inc(s_oT_pe, TILES - 2)
            pe.sem_inc(s_wo_pe, TILES - 3)
            run_steps(pe, step)
            END = BATCH * KV
            for h in range(GROUP):
                weigh(END - 1, TILES - 1, h, (END - 1) % 2)
            ring2_read(END, 0)
            turn_o(END - 1, TILES - 2)
            out_project(END - 1, KV - 1, TILES - 3)
            ring2_read(END, 1)
            turn_o(END - 1, TILES - 1)
            out_project(END - 1, KV - 1, TILES - 2)
            out_project(END - 1, KV - 1, TILES - 1)


def kernel(L0_attn_hidden_states, L0_attn_Wq, L0_attn_bq, L0_attn_Wk, L0_attn_bk, L0_attn_Wv, L0_attn_bv, L0_attn_Wo,
           L0_attn_bo, L0_attn_sinks, L0_ffn_weight, L0_ffn_weight_scale, L0_ffn_bias):
    import concourse.bacc as bacc
    from concourse.bass_utils import run_bass_kernel_spmd

    def host(a):
        return np.asarray(a)

    wq = host(L0_attn_Wq).reshape(KT, P, KV, QW)
    wk = host(L0_attn_Wk).reshape(KT, P, KV, D)
    wv = host(L0_attn_Wv).reshape(KT, P, KV, D)
    w_qkv = np.concatenate([wq, wk, wv], axis=3).reshape(KT, P, KV * PW)
    b_qkv = np.concatenate([host(L0_attn_bq).reshape(KV, QW), host(L0_attn_bk), host(L0_attn_bv)], axis=1).reshape(-1)
    w_o = host(L0_attn_Wo).reshape(KV * KT, P, M).transpose(1, 0, 2).reshape(P, KV * KT * M)
    w_ffn = host(L0_ffn_weight).T.reshape(KT, P, M).transpose(1, 0, 2).reshape(P, KT * M)

    inv_freq = np.float32(1.0) / np.float32(WAVELENGTH) ** (np.arange(D // 2, dtype=np.float32) * np.float32(2.0) / D)
    freqs = np.arange(SEQ, dtype=np.float32)[:, None] * inv_freq.astype(np.float32)[None, :]
    c, sn = np.cos(freqs) * np.float32(SCALE), np.sin(freqs) * np.float32(SCALE)
    cos = np.repeat(c, 2, axis=1).reshape(TILES, P, D).transpose(1, 0, 2)
    sin = np.stack([-sn, sn], axis=-1).reshape(TILES, P, D).transpose(1, 0, 2)

    arrays = {"x": host(L0_attn_hidden_states), "w_qkv": w_qkv, "b_qkv": b_qkv, "w_o": w_o, "b_o": host(L0_attn_bo),
              "sinks": host(L0_attn_sinks), "w_ffn": w_ffn, "w_scale": host(L0_ffn_weight_scale).reshape(1),
              "b_ffn": host(L0_ffn_bias), "rope_cos": cos.astype(np.float32), "rope_sin": sin.astype(np.float32)}
    arrays = {f"in_{n}": np.ascontiguousarray(a) for n, a in arrays.items()}
    nc = bacc.Bacc("TRN2", target_bir_lowering=False, num_devices=1)
    args = [nc.dram_tensor(n, a.shape, mybir.dt.from_np(a.dtype), kind="ExternalInput").ap()
            for n, a in arrays.items()]
    out = nc.dram_tensor("out", (BATCH, SEQ, M), F32, kind="ExternalOutput").ap()
    gated_window_attention(nc, *args, out)
    result = run_bass_kernel_spmd(nc, [arrays], core_ids=[0])
    return result.results[0]["out"]
```

```python
from contextlib import ExitStack

import numpy as np
import concourse.bass as bass
import concourse.mybir as mybir

F32 = mybir.dt.float32
F32R = mybir.dt.float32r
BF16 = mybir.dt.bfloat16
U32 = mybir.dt.uint32
ALU = mybir.AluOpType
ACT = mybir.ActivationFunctionType
AX = mybir.AxisListType

P = 128
BATCH, SEQ, M = 8, 512, 256
HEADS, KV, D = 32, 8, 64
GROUP = HEADS // KV
TILES = SEQ // P
KT = M // P
QW = GROUP * D
ROT = QW + D
PW = ROT + D
HW = 2 * D
NR = 2 * GROUP
QKW = GROUP * HW + 3 * D
DV = D + 1
WINDOW = 128
WAVELENGTH = 150000.0
SCALE = D ** -0.25
LN_EPS = 1e-5
FP8_MAX, SCALE_EPS = 448.0, 1e-7
MASKED = -1e30
LOWEST = -3e38
EXPONENT_BITS = 0x7F800000
FP8_MIN_NORMAL = 2.0 ** -6
ROUND_TO_4_BITS = 1.5 * 2.0 ** 20
NP = 6
SIGMOID_LOWEST = -87.0
CHUNK = 1536
W_CHUNKS, O_CHUNKS = 2 * KT, 4
N_CHUNKS = W_CHUNKS + O_CHUNKS + 1

BLOCKS = [[k for k in (t - 1, t + 1, t) if 0 <= k < TILES] for t in range(TILES)]
FIRST = [sum(len(b) for b in BLOCKS[:t]) for t in range(TILES + 1)]
CUT = [sum(len(b) - 1 for b in BLOCKS[:t]) for t in range(TILES + 1)]
NB, NCUT = FIRST[-1], CUT[-1]


def at(eng, sem, per, step, k):
    if isinstance(step, int) and per * step + k <= 0:
        return
    eng.wait_ge(sem, step * per + k)


def stand_apart(eng, passed):
    eng.sem_inc(passed, 1)


def back(step, q, n):
    return (step, q - n) if q >= n else (step - 1, q - n + TILES)


def of_group(tensor, group, width):
    return tensor[:, group * width:(group + 1) * width] if isinstance(group, int) else \
        tensor[:, bass.ds(group * width, width)]


def filling(k, q):
    return (k + 2) * TILES + q if k is not None and k < 0 else None


def run_steps(eng, step, first):
    step(-2, 0, (0, None, None, None), k=-2)
    step(-1, 1, (1, 0, None, None), k=-1)
    first()
    with eng.Fori(0, BATCH) as n:
        for k in (0, 1):
            step(n * KV + k, k, (k + 2, k + 1, k, (k - 1) % KV), n, k)
        with eng.Fori(1, KV // 2 - 1) as pair:
            for k in (0, 1):
                g = pair * 2 + k
                step(n * KV + g, k, (g + 2, g + 1, g, g - 1), n, k + 2, pair - 1)
        for k in (KV - 2, KV - 1):
            step(n * KV + k, k % 2, ((k + 2) % KV, (k + 1) % KV, k, k - 1), n, k)


def gated_window_attention(nc, x, w_qkv, b_qkv, w_o, b_o, sinks, w_ffn, w_scale, b_ffn, rope_cos, rope_sin, out):
    x_t = x.rearrange("b (t p) m -> b p t m", p=P)
    out_t = out.rearrange("b (t p) m -> b p t m", p=P)

    with ExitStack() as ctx:
        def sb(name, shape, dt):
            return ctx.enter_context(nc.sbuf_tensor(name, shape, dt))

        w_hi = sb("w_hi", [P, KT, KV * PW], F32R)
        w_lo = sb("w_lo", [P, KT, KV * PW], F32R)
        wo_hi = sb("wo_hi", [P, KV * KT * M], F32R)
        wo_lo = sb("wo_lo", [P, KV * KT * M], F32R)
        ffn_hi = sb("ffn_hi", [P, KT * M], F32R)
        ffn_lo = sb("ffn_lo", [P, KT * M], F32R)
        bias = sb("bias", [P, KV * PW], F32)
        ffn_bias = sb("ffn_bias", [P, M], F32)
        out_bias = sb("out_bias", [P, M], F32)
        cos = sb("cos", [P, TILES, D], F32)
        sin = sb("sin", [P, TILES, D], F32)
        neg_sink = sb("neg_sink", [P, HEADS], F32)
        scale_w = sb("scale_w", [P, 1], F32)
        ident = sb("ident", [P, P], F32)
        ident_r = sb("ident_r", [P, P], F32R)
        ident_b = sb("ident_b", [P, P], BF16)
        ones = sb("ones", [1, P], F32)
        mask = sb("mask", [P, 3 * P], F32)
        eps = sb("eps", [P, TILES], F32)
        minus_half = sb("minus_half", [P, TILES], F32)
        x_in = sb("x_in", [P, TILES, M], F32)
        x_res = sb("x_res", [P, 2, M], F32)
        xn = sb("xn", [P, TILES, M], F32)
        xq = xn[:, :, :].bitcast(BF16)[:, :, 0:M]
        xT_hi = sb("xT_hi", [P, KT, SEQ], F32R)
        xT_lo = sb("xT_lo", [P, KT, SEQ], F32R)
        xqT = sb("xqT", [P, KT, SEQ], F32R)
        gate = sb("gate", [P, TILES, M], F32)
        ffn_e = sb("ffn_e", [P, 2, M], F32)
        stats = sb("stats", [P, TILES, 6], F32)
        moments = sb("moments", [P, TILES, 2], F32)
        var_eps = sb("var_eps", [P, TILES], F32)
        rstd = sb("rstd", [P, TILES], F32)
        absmax = sb("absmax", [P, BATCH], F32)
        amax = sb("amax", [P, 1], F32)
        scale_row = sb("scale_row", [1, 4], F32)
        inv_scale = sb("inv_scale", [P, 1], F32)
        proj = sb("proj", [P, 2, PW], F32)
        turn_s = sb("turn_s", [P, ROT], F32)
        turned = sb("turned", [P, 2, ROT], F32)
        qk_parts = sb("qk_parts", [P, 2, TILES, QKW], F32R)
        v_new = sb("v_new", [P, TILES, D], F32)
        v = sb("v", [P, 2, TILES, DV], F32)
        qT_full = sb("qT_full", [P, TILES, GROUP * P], F32R)
        qT_high = sb("qT_high", [P, TILES, GROUP * P], F32R)
        neg_parts = sb("neg_parts", [P, TILES, NR], F32R)
        own_rows = sb("own_rows", [NR, GROUP], F32)
        kT_high = sb("kT_high", [P, 2, SEQ], F32R)
        kT_low = sb("kT_low", [P, 2, SEQ], F32R)
        junk = sb("junk", [P, 2, 3 * P], BF16)
        row_max = sb("row_max", [P, GROUP], F32)
        neg_max = sb("neg_max", [P, GROUP], F32)
        sink_arg = sb("sink_arg", [P, TILES, GROUP], F32)
        sink_exp = sb("sink_exp", [P, 2, TILES, GROUP], F32)
        stage = sb("stage", [P, 2 * CHUNK], F32)
        prob = stage[:, 0:NP * GROUP * P].rearrange("p (s n) -> p s n", s=NP)
        den = sb("den", [P, GROUP], F32)
        rden = sb("rden", [P, GROUP], F32)
        o_norm = sb("o_norm", [P, GROUP, D], F32)
        oT_hi = sb("oT_hi", [P, 2, KT * P], F32R)
        oT_lo = sb("oT_lo", [P, 2, KT * P], F32R)

        def bank(name):
            return ctx.enter_context(nc.psum_tensor(name, [P, 512], F32))

        ring = [bank(f"ring{i}") for i in range(3)]
        score = [bank(f"score{i}") for i in range(2)]
        pv_bank = bank("pv_bank")
        acc = [bank(f"acc{i}") for i in range(2)]
        pv = pv_bank[:, 0:GROUP * DV].rearrange("p (h d) -> p h d", h=GROUP)

        def sem(name):
            return ctx.enter_context(nc.semaphore(name))

        s_const_in = sem("const_in")
        s_bias_in = sem("bias_in")
        s_id_memset = sem("id_memset")
        s_id_ready = sem("id_ready")
        s_rows_self = sem("rows_self")
        s_ones_ready = sem("ones_ready")
        s_w_hi_done = sem("w_hi_done")
        s_w_lo_done = sem("w_lo_done")
        s_w_scaled = sem("w_scaled")
        s_x_got = sem("x_got")
        s_x_odd_got = sem("x_odd_got")
        s_res_got = sem("res_got")
        s_out_put = sem("out_put")
        s_ln_bn = sem("ln_bn")
        s_ln_stat = sem("ln_stat")
        s_ln_eps = sem("ln_eps")
        s_ln_rstd = sem("ln_rstd")
        s_xn_done = sem("xn_done")
        s_ln_done = sem("ln_done")
        s_amax_done = sem("amax_done")
        s_amax_pe = sem("amax_pe")
        s_amax_self = sem("amax_self")
        s_scale_pe = sem("scale_pe")
        s_inv_ready = sem("inv_ready")
        s_sink_negated = sem("sink_negated")
        s_quant_self = sem("quant_self")
        s_x_scaled = sem("x_scaled")
        s_xq_done = sem("xq_done")
        s_ffn_pe = sem("ffn_pe")
        s_ffn_z = sem("ffn_z")
        s_ffn_clamped = sem("ffn_clamped")
        s_ffn_exp = sem("ffn_exp")
        s_ffn_sum = sem("ffn_sum")
        s_ffn_inverse = sem("ffn_inverse")
        s_gate_done = sem("gate_done")
        s_xT_pe = sem("xT_pe")
        s_xT_hi_done = sem("xT_hi_done")
        s_xT_lo_done = sem("xT_lo_done")
        s_xqT_pe = sem("xqT_pe")
        s_xqT_done = sem("xqT_done")
        s_fin_read = sem("fin_read")
        s_gated = sem("gated")
        s_fin_done = sem("fin_done")
        s_proj_pe = sem("proj_pe")
        s_proj_done = sem("proj_done")
        s_turn_self = sem("turn_self")
        s_turned_done = sem("turned_done")
        s_hi_done = sem("hi_done")
        s_lo_done = sem("lo_done")
        s_v_new_done = sem("v_new_done")
        s_v_ready = sem("v_ready")
        s_qfull_pe = sem("qfull_pe")
        s_qfull_done = sem("qfull_done")
        s_kT_pe = sem("kT_pe")
        s_kT_done = sem("kT_done")
        s_max_turned_pe = sem("max_turned_pe")
        s_qhigh_done = sem("qhigh_done")
        s_max_rows_done = sem("max_rows_done")
        s_max_pe = sem("max_pe")
        s_max_done = sem("max_done")
        s_small_self = sem("small_self")
        s_mh_done = sem("mh_done")
        s_neg_done = sem("neg_done")
        s_sink_done = sem("sink_done")
        s_score_pe = sem("score_pe")
        s_exp_done = sem("exp_done")
        s_cut_done = sem("cut_done")
        s_pv_pe = sem("pv_pe")
        s_norm_self = sem("norm_self")
        s_norm_done = sem("norm_done")
        s_oT_pe = sem("oT_pe")
        s_oT_hi_done = sem("oT_hi_done")
        s_oT_lo_done = sem("oT_lo_done")
        s_wo_pe = sem("wo_pe")
        s_dve_passed = sem("dve_passed")
        s_pool_passed = sem("pool_passed")
        s_sp_passed = sem("sp_passed")
        stage_in = [ctx.enter_context(nc.semaphore(f"stage_in{j}")) for j in range(2)]
        block = ctx.enter_context(nc.Block())

        consts = [(scale_w[:, :], w_scale.partition_broadcast(P)), (neg_sink[:, :], sinks.partition_broadcast(P)),
                  (cos[:, :, :], rope_cos), (sin[:, :, :], rope_sin), (ffn_bias[:, :], b_ffn.partition_broadcast(P)),
                  (out_bias[:, :], b_o.partition_broadcast(P)),
                  (bias[:, 0:2 * PW], b_qkv[0:2 * PW].partition_broadcast(P))]

        half = KV * PW // 2
        chunks = [(w_qkv[k, :, j * half:(j + 1) * half], w_hi[:, k, j * half:(j + 1) * half],
                   w_lo[:, k, j * half:(j + 1) * half]) for k in range(KT) for j in range(2)]
        chunks.append((w_ffn, ffn_hi[:, :], ffn_lo[:, :]))
        wide = KV * KT * M // O_CHUNKS
        chunks += [(w_o[:, j * wide:(j + 1) * wide], wo_hi[:, j * wide:(j + 1) * wide],
                    wo_lo[:, j * wide:(j + 1) * wide]) for j in range(O_CHUNKS)]
        FFN_CHUNK = W_CHUNKS

        def staged(n):
            width = chunks[n][1].shape[-1]
            return stage[:, (n % 2) * CHUNK:(n % 2) * CHUNK + width]

        @block.sync
        def _(sp):
            def load_x(n):
                if n >= 2:
                    sp.wait_ge(s_ln_done, n - 1)
                buf, got = (x_in, s_x_got) if n % 2 == 0 else (gate, s_x_odd_got)
                sp.dma_start(buf[:, :, :], x_t[n % BATCH]).then_inc(got, 16)

            def load_chunk(n):
                if n >= 2:
                    sp.wait_ge(s_w_lo_done, n - 1)
                sp.dma_start(staged(n), chunks[n][0]).then_inc(stage_in[n % 2], 16)

            load_x(0)
            load_chunk(0)
            load_chunk(1)
            for dst, src in consts:
                sp.dma_start(dst, src).then_inc(s_const_in, 16)
            load_x(1)
            for n in range(2, W_CHUNKS + 1):
                load_chunk(n)
            load_x(2)
            load_chunk(W_CHUNKS + 1)
            for n in range(3, BATCH + 1):
                load_x(n)
                if n + W_CHUNKS - 1 < N_CHUNKS:
                    load_chunk(n + W_CHUNKS - 1)
            sp.dma_start(bias[:, 2 * PW:], b_qkv[2 * PW:].partition_broadcast(P)).then_inc(s_bias_in, 16)
            sp.wait_ge(s_xq_done, 2)
            sp.dma_start(x_in[:, :, :], x_t[1]).then_inc(s_x_got, 16)

            def result(n, j, x_b, out_b):
                sp.dma_start(x_res[:, :, :], x_b[:, 2 * j:2 * j + 2, :]).then_inc(s_res_got, 16)
                sp.wait_ge(s_fin_done, n * 2 + (j + 1))
                if out_b is not None:
                    sp.dma_start(out_b[:, 2 * j:2 * j + 2, :], x_res[:, :, :]).then_inc(s_out_put, 16)
                    sp.wait_ge(s_out_put, n * 32 + (16 * j - 16))
                    if not isinstance(n, int):
                        stand_apart(sp, s_sp_passed)

            result(0, 0, x_t[0], None)
            result(0, 1, x_t[0], None)
            sp.wait_ge(s_xq_done, 4)
            sp.dma_start(x_in[:, :, :], x_t[2]).then_inc(s_x_got, 16)
            with sp.Fori(1, BATCH - 2) as n:
                for j in range(2):
                    result(n, j, x_t[bass.ds(n - 1, 1)][0], out_t[bass.ds(n - 1, 1)][0])
                sp.wait_ge(s_xq_done, n * 2 + 4)
                sp.dma_start(x_in[:, :, :], x_t[bass.ds(n + 2, 1)][0]).then_inc(s_x_got, 16)
            for n in range(BATCH - 2, BATCH + 1):
                for j in range(2):
                    result(n, j, x_t[n - 1], out_t[n - 1])
                if n == BATCH - 2:
                    sp.wait_ge(s_xq_done, 2 * BATCH)
                    sp.dma_start(x_in[:, :, :], x_t[0]).then_inc(s_x_got, 16)
            sp.wait_ge(s_x_got, 16 * (BATCH // 2 + BATCH + 1))

        @block.gpsimd
        def _(pool):
            nc.gpsimd.memset(ident[:, :], 0.0).then_inc(s_id_memset, 1)
            nc.gpsimd.memset(mask[:, :], 0.0).then_inc(s_id_memset, 1)
            nc.gpsimd.memset(eps[:, :], LN_EPS).then_inc(s_id_memset, 1)
            nc.gpsimd.memset(minus_half[:, :], -0.5).then_inc(s_id_memset, 1)
            nc.gpsimd.memset(v[:, :, :, :], 1.0).then_inc(s_id_memset, 1)
            nc.gpsimd.memset(ones[:, :], 1.0).then_inc(s_ones_ready, 1)
            nc.gpsimd.memset(own_rows[:, :], 1.0).then_inc(s_id_memset, 1)
            nc.gpsimd.memset(o_norm[:, :, :], 0.0).then_inc(s_norm_done, TILES - 1)
            nc.gpsimd.memset(sink_exp[:, :, :, :], 1.0).then_inc(s_sink_done, TILES)
            nc.gpsimd.memset(oT_hi[:, :, :].bitcast(F32), 0.0).then_inc(s_oT_hi_done, TILES - 2)
            nc.gpsimd.memset(oT_lo[:, :, :].bitcast(F32), 0.0).then_inc(s_oT_lo_done, TILES - 2)
            pool.sem_inc(s_cut_done, NCUT)
            pool.wait_ge(s_id_memset, 6)
            nc.gpsimd.affine_select(out=ident[:, :], in_=ident[:, :], compare_op=ALU.not_equal, fill=1.0, base=0,
                                    pattern=[[-1, P]], channel_multiplier=1).then_inc(s_id_ready, 1)
            nc.gpsimd.affine_select(out=own_rows[:, :], in_=own_rows[:, :], compare_op=ALU.is_ge, fill=0.0, base=0,
                                    pattern=[[-2, GROUP]], channel_multiplier=1).then_inc(s_rows_self, 1)
            pool.wait_ge(s_rows_self, 1)
            nc.gpsimd.affine_select(out=own_rows[:, :], in_=own_rows[:, :], compare_op=ALU.is_ge, fill=0.0, base=1,
                                    pattern=[[2, GROUP]], channel_multiplier=-1).then_inc(s_id_ready, 1)
            nc.gpsimd.affine_select(out=mask[:, 0:P], in_=mask[:, 0:P], compare_op=ALU.is_ge, fill=MASKED, base=0,
                                    pattern=[[1, P]], channel_multiplier=-1).then_inc(s_id_ready, 1)
            nc.gpsimd.affine_select(out=mask[:, 2 * P:], in_=mask[:, 2 * P:], compare_op=ALU.is_ge, fill=MASKED,
                                    base=0, pattern=[[-1, P]], channel_multiplier=1).then_inc(s_id_ready, 1)

            def rstd_of(n):
                pool.wait_ge(s_ln_stat, n + 1)
                nc.gpsimd.tensor_tensor(var_eps[:, :], moments[:, :, 1], eps[:, :], ALU.add).then_inc(s_ln_eps, 1)
                pool.wait_ge(s_ln_eps, n + 1)
                nc.gpsimd.tensor_tensor(rstd[:, :], var_eps[:, :], minus_half[:, :], ALU.pow).then_inc(s_ln_rstd, 1)

            def turn(a, q):
                slot = q % 2
                at(pool, s_proj_done, TILES, a, q + 1)
                at(pool, s_turned_done, TILES, a, q)
                at(pool, s_lo_done, TILES, a, q - 1)
                x_qk = proj[:, slot, 0:ROT]
                cos_q = cos[:, q, :].rearrange("p (a d) -> p a d", a=1).broadcast_to([P, GROUP + 1, D])
                sin_q = sin[:, q, :].rearrange("p (a i t) -> p a i t", a=1, t=2) \
                    .broadcast_to([P, GROUP + 1, D // 2, 2])
                nc.gpsimd.tensor_tensor(turned[:, slot, :].rearrange("p (h d) -> p h d", d=D),
                                        x_qk.rearrange("p (h d) -> p h d", d=D), cos_q, ALU.mult) \
                    .then_inc(s_turn_self, 1)
                nc.gpsimd.tensor_tensor(turn_s[:, :].rearrange("p (h i t) -> p h i t", i=D // 2, t=2),
                                        x_qk.rearrange("p (h i t) -> p h i t", i=D // 2, t=2)[:, :, :, ::-1],
                                        sin_q, ALU.mult).then_inc(s_turn_self, 1)
                at(pool, s_turn_self, 2 * TILES, a, 2 * q + 2)
                nc.gpsimd.tensor_tensor(turned[:, slot, :], turned[:, slot, :], turn_s[:, :], ALU.add) \
                    .then_inc(s_turned_done, 1)

            def split_lo(a, q, par):
                at(pool, s_hi_done, 2 * TILES, a, 2 * q + 2)
                parts = qk_parts[:, par, q, 0:(GROUP + 1) * HW].rearrange("p (h w) -> p h w", w=HW)
                nc.gpsimd.tensor_tensor(parts[:, :, 0:D], turned[:, q % 2, :].rearrange("p (h d) -> p h d", d=D),
                                        parts[:, :, D:2 * D].bitcast(F32), ALU.subtract).then_inc(s_lo_done, 1)

            def finish(n, j):
                pool.wait_ge(s_gated, n * 2 + (j + 1))
                pool.wait_ge(s_res_got, n * 32 + (16 * j + 16))
                nc.gpsimd.tensor_tensor(x_res[:, :, :], x_res[:, :, :], gate[:, 2 * j:2 * j + 2, :], ALU.add) \
                    .then_inc(s_fin_done, 1)

            def cut(c, q):
                for n, k in enumerate(BLOCKS[q]):
                    if k == q:
                        continue
                    at(pool, s_exp_done, NB, c + 1, FIRST[q] + n + 1)
                    sign = 1 if k > q else -1
                    pr = prob[:, q % 2 * 3 + n, :].rearrange("p (h n) -> p h n", h=GROUP)
                    stand_apart(pool, s_pool_passed)
                    nc.gpsimd.affine_select(out=pr, in_=pr, compare_op=ALU.is_ge, fill=0.0, base=0,
                                            pattern=[[0, GROUP], [sign, P]], channel_multiplier=-sign) \
                        .then_inc(s_cut_done, 1)

            def step(it, par, groups, n=None, k=None, half=None):
                for q in range(TILES):
                    if groups[2] is not None:
                        cut(it, q)
                    fill = filling(k, q)
                    if fill is not None and fill + 2 <= BATCH:
                        rstd_of(fill + 2)
                    if (k, q) == (0, 2):
                        rstd_of(n + (BATCH + 1))
                    if (k, q) in ((0, 1), (0, 3)):
                        finish(n, q // 2)
                    if q >= 1 or groups[1] is not None:
                        split_lo(*back(it + 2, q, 1), par if q >= 1 else 1 - par)
                    turn(it + 2, q)

            rstd_of(0)
            rstd_of(1)
            run_steps(pool, step, first=lambda: None)
            finish(BATCH, 0)
            finish(BATCH, 1)

        @block.scalar
        def _(act):
            def chunk_high(n):
                act.wait_ge(stage_in[n % 2], 16 * (n // 2 + 1))
                if n == FFN_CHUNK:
                    act.wait_ge(s_const_in, 16 * len(consts))
                    nc.scalar.activation(staged(n), staged(n), ACT.Copy, scale=scale_w[:, 0:1]).then_inc(s_w_scaled, 1)
                    act.wait_ge(s_w_scaled, 1)
                nc.scalar.activation(chunks[n][1], staged(n), ACT.Copy).then_inc(s_w_hi_done, 1)

            act.wait_ge(s_id_ready, 4)
            nc.scalar.activation(ident_b[:, :], ident[:, :], ACT.Copy).then_inc(s_id_ready, 1)
            nc.scalar.activation(ident_r[:, :], ident[:, :], ACT.Copy).then_inc(s_id_ready, 1)
            act.sem_inc(s_exp_done, NB)

            def x_high(n, k):
                act.wait_ge(s_xT_pe, n * KT + (k + 1))
                nc.scalar.activation(xT_hi[:, k, :], ring[2 - k][:, :], ACT.Copy).then_inc(s_xT_hi_done, 1)

            def xq_turned(n, k):
                act.wait_ge(s_xqT_pe, n * KT + (k + 1))
                nc.scalar.activation(xqT[:, k, :], ring[2][:, :], ACT.Copy).then_inc(s_xqT_done, 1)

            def scale_x(n):
                act.wait_ge(s_xn_done, n + (BATCH + 1))
                nc.scalar.activation(x_in[:, :, :], xn[:, :, :], ACT.Copy, scale=inv_scale[:, 0:1]) \
                    .then_inc(s_x_scaled, 1)

            def ffn_exp(b, j):
                act.wait_ge(s_ffn_clamped, b * 2 + j + 1)
                nc.scalar.activation(ffn_e[:, :, :], ffn_e[:, :, :], ACT.Exp, scale=-1.0) \
                    .then_inc(s_ffn_exp, 1)

            def exps(c, q, n):
                at(act, s_score_pe, NB, c, FIRST[q] + n + 1)
                nc.scalar.activation(prob[:, q % 2 * 3 + n, :], score[(FIRST[q] + n) % 2][:, :], ACT.Exp) \
                    .then_inc(s_exp_done, 1)

            def q_full(b, q):
                at(act, s_qfull_pe, TILES, b, q + 1)
                nc.scalar.activation(qT_full[:, q, :], ring[0][:, :], ACT.Copy).then_inc(s_qfull_done, 1)

            def q_high(b, q):
                at(act, s_qfull_done, TILES, b, q + 1)
                nc.scalar.activation(qT_high[0:D, q, :], qT_full[D:2 * D, q, :].bitcast(F32), ACT.Copy) \
                    .then_inc(s_qhigh_done, 1)

            def k_turned(b, par, low):
                at(act, s_kT_pe, 2, b, 1 + low)
                if low:
                    nc.scalar.activation(kT_low[0:D, par, :], ring[2][0:D, :], ACT.Copy).then_inc(s_kT_done, 1)
                else:
                    nc.scalar.activation(kT_high[:, par, :], ring[2][:, :], ACT.Copy).then_inc(s_kT_done, 1)

            def max_rows(b, q, par):
                at(act, s_max_turned_pe, TILES, b, q + 1)
                for h in range(GROUP):
                    last = nc.scalar.activation(qT_high[D:D + NR, q, h * P:(h + 1) * P], ring[2][0:NR, 0:P],
                                                ACT.Copy, scale=own_rows[:, h:h + 1])
                last.then_inc(s_max_rows_done, 1)
                nc.scalar.activation(sink_exp[:, par, q, :], sink_arg[:, q, :], ACT.Exp).then_inc(s_sink_done, 1)

            def split_hi(a, q, par):
                at(act, s_turned_done, TILES, a, q + 1)
                parts = qk_parts[:, par, q, 0:(GROUP + 1) * HW].rearrange("p (h w) -> p h w", w=HW)
                nc.scalar.activation(parts[:, :, D:2 * D], turned[:, q % 2, :].rearrange("p (h d) -> p h d", d=D),
                                     ACT.Copy).then_inc(s_hi_done, 1)
                nc.scalar.activation(qk_parts[:, par, q, QKW - D:QKW], turned[:, q % 2, QW:ROT], ACT.Copy) \
                    .then_inc(s_hi_done, 1)

            def v_aside(a, q):
                at(act, s_v_ready, 1, a, 0)
                nc.scalar.activation(v_new[:, q, :], proj[:, q % 2, ROT:PW], ACT.Copy).then_inc(s_v_new_done, 1)

            def keep_v(b, par):
                at(act, s_v_new_done, TILES, b, TILES)
                at(act, s_pv_pe, TILES, b - 1, TILES)
                nc.scalar.activation(v[:, par, :, 0:D], v_new[:, :, :], ACT.Copy).then_inc(s_v_ready, 1)

            def o_high(c, q):
                at(act, s_oT_pe, TILES, c + 1, q + 1)
                nc.scalar.activation(oT_hi[:, q % 2, :], ring[2][:, 0:KT * P], ACT.Copy).then_inc(s_oT_hi_done, 1)

            def step(it, par, groups, n=None, k=None, half=None):
                _, b, c, _ = groups
                for q in range(TILES):
                    b1 = (b if q >= 1 else c) is not None
                    b2 = (b if q >= 2 else c) is not None
                    if c is not None:
                        exps(it, q, 0)
                    if b is not None and q == 1:
                        k_turned(it + 1, 1 - par, 0)
                        q_full(it + 1, 0)
                    if c is not None:
                        exps(it, q, 1)
                    if k == KV - 1 and q >= 2:
                        xq_turned(n + 1, q - 2)
                    if b1 and q != 1:
                        q_full(*back(it + 1, q, 1))
                    if (k, q) == (KV - 2, 0):
                        x_high(n + 1, 0)
                        x_high(n + 1, 1)
                    if b is not None and q == 1:
                        k_turned(it + 1, 1 - par, 1)
                    if q >= 1 or b is not None:
                        a_step, a_tile = back(it + 2, q, 1)
                        a_par = par if q >= 1 else 1 - par
                        split_hi(a_step, a_tile, a_par)
                        if q == 1 and b is not None:
                            keep_v(it + 1, 1 - par)
                        v_aside(a_step, a_tile)
                    if b2:
                        max_rows(*back(it + 1, q, 2), 1 - par if q >= 2 else par)
                    if c is not None and len(BLOCKS[q]) > 2:
                        exps(it, q, 2)
                    if c is not None and q != 1:
                        o_high(*back(it, q, 2))
                    if b1:
                        q_high(*back(it + 1, q, 1))
                    if c is not None and q == 1:
                        o_high(*back(it, q, 2))
                    fill = filling(k, q)
                    if fill is not None and W_CHUNKS + fill < N_CHUNKS:
                        chunk_high(W_CHUNKS + fill)
                    if (k, q) == (2, 0):
                        ffn_exp(n, half)
                    if (k, q) == (KV - 2, 0):
                        scale_x(n + 1)

            chunk_high(0)
            chunk_high(1)
            for k in range(KT):
                x_high(0, k)
            for n in range(2, W_CHUNKS):
                chunk_high(n)

            def first():
                act.wait_ge(s_inv_ready, 1)
                scale_x(0)
                for k in range(KT):
                    xq_turned(0, k)

            run_steps(act, step, first)
            for q in range(2):
                o_high(*back(BATCH * KV, q, 2))

        @block.vector
        def _(dve):
            def statistics(n, buf, tiles):
                for t in tiles:
                    nc.vector.bn_stats(stats[:, t, :], buf[:, t, :]).then_inc(s_ln_bn, 1)

            def moments_of(n):
                at(dve, s_xn_done, 1, n, 0)
                for t in range(TILES):
                    at(dve, s_ln_bn, TILES, n, t + 1)
                    stand_apart(dve, s_dve_passed)
                    last = nc.vector.bn_aggr(moments[:, t, :], stats[:, t, :])
                last.then_inc(s_ln_stat, 1)

            def normalise(n, buf, tiles):
                at(dve, s_ln_rstd, 1, n, 1)
                at(dve, s_xqT_pe, KT, n - (BATCH + 1), KT)
                for t in tiles:
                    last = nc.vector.tensor_scalar(xn[:, t, :], buf[:, t, :], moments[:, t, 0:1], rstd[:, t:t + 1],
                                                   ALU.subtract, ALU.mult)
                if TILES - 1 in tiles:
                    last.then_inc(s_xn_done, 1)

            def measure(n):
                dve.wait_ge(s_xn_done, n + 1)
                nc.vector.tensor_reduce(absmax[:, n:n + 1], xn[:, :, :], AX.XY, ALU.max,
                                        apply_absolute_value=True).then_inc(s_ln_done, 1)

            def chunk_low(n):
                dve.wait_ge(s_w_hi_done, n + 1)
                _, hi, lo = chunks[n]
                nc.vector.tensor_tensor(lo, staged(n), hi.bitcast(F32), ALU.subtract).then_inc(s_w_lo_done, 1)

            def exponents(n, j):
                at(dve, s_x_scaled, 1, n, 1)
                if j:
                    at(dve, s_xq_done, 2, n, 1)
                val, big = x_in[:, 2 * j:2 * j + 2, :], ffn_e[:, :, :]
                nc.vector.tensor_scalar(big.bitcast(U32), val.bitcast(U32), EXPONENT_BITS, None,
                                        ALU.bitwise_and).then_inc(s_quant_self, 1)
                at(dve, s_quant_self, 6, n, 3 * j + 1)
                nc.vector.tensor_scalar(big, big, FP8_MIN_NORMAL, ROUND_TO_4_BITS, ALU.max, ALU.mult) \
                    .then_inc(s_quant_self, 1)

            def quantise(n, j):
                val, big = x_in[:, 2 * j:2 * j + 2, :], ffn_e[:, :, :]
                at(dve, s_quant_self, 6, n, 3 * j + 2)
                nc.vector.tensor_tensor(val, val, big, ALU.add).then_inc(s_quant_self, 1)
                at(dve, s_quant_self, 6, n, 3 * j + 3)
                nc.vector.tensor_tensor(xq[:, 2 * j:2 * j + 2, :], val, big, ALU.subtract).then_inc(s_xq_done, 1)

            def x_low(n, k):
                at(dve, s_xT_hi_done, KT, n, k + 1)
                nc.vector.tensor_tensor(xT_lo[:, k, :], ring[2 - k][:, :], xT_hi[:, k, :].bitcast(F32),
                                        ALU.subtract).then_inc(s_xT_lo_done, 1)

            def ffn_bias_on(b, j):
                dve.wait_ge(s_fin_done, b * 2 + (j + 1))
                dve.wait_ge(s_ffn_pe, b * 2 + (j + 1))
                nc.vector.tensor_tensor(gate[:, 2 * j:2 * j + 2, :],
                                        ring[2][:, :].rearrange("p (t m) -> p t m", t=2),
                                        ffn_bias[:, :].rearrange("p (a m) -> p a m", a=1)
                                        .broadcast_to([P, 2, M]), ALU.add).then_inc(s_ffn_z, 1)

            def ffn_clamp(b, j):
                dve.wait_ge(s_ffn_z, b * 2 + 2)
                dve.wait_ge(s_xq_done, b * 2 + 2)
                dve.wait_ge(s_gate_done, b * 2 + j + 2)
                nc.vector.tensor_scalar(ffn_e[:, :, :], gate[:, bass.ds(j * 2, 2), :], SIGMOID_LOWEST, None,
                                        ALU.max).then_inc(s_ffn_clamped, 1)

            def ffn_one_more(b, j):
                dve.wait_ge(s_ffn_exp, b * 2 + j + 1)
                nc.vector.tensor_scalar(ffn_e[:, :, :], ffn_e[:, :, :], 1.0, None, ALU.add).then_inc(s_ffn_sum, 1)

            def ffn_invert(b, j, part):
                if part == 0:
                    dve.wait_ge(s_ffn_sum, b * 2 + j + 1)
                e = ffn_e[:, part // 2, part % 2 * P:(part % 2 + 1) * P]
                nc.vector.reciprocal(e, e).then_inc(s_ffn_inverse, 1)

            def ffn_gate(b, j):
                dve.wait_ge(s_ffn_inverse, b * 8 + j * 4 + 4)
                pair = gate[:, bass.ds(j * 2, 2), :]
                nc.vector.tensor_tensor(pair, pair, ffn_e[:, :, :], ALU.mult).then_inc(s_gate_done, 1)

            def gated(n, j):
                if j == 0:
                    dve.wait_ge(s_gate_done, n * 2 + 2)
                dve.wait_ge(s_wo_pe, n * (TILES * KV) + (2 + 2 * j))
                pair = gate[:, 2 * j:2 * j + 2, :]
                sums = ffn_e[:, :, :]
                nc.vector.tensor_tensor(sums, acc[j][:, :].rearrange("p (t m) -> p t m", t=2),
                                        out_bias[:, :].rearrange("p (a m) -> p a m", a=1).broadcast_to([P, 2, M]),
                                        ALU.add).then_inc(s_fin_read, 1)
                dve.wait_ge(s_fin_read, n * 2 + j + 1)
                nc.vector.tensor_tensor(pair, sums, pair, ALU.mult).then_inc(s_gated, 1)

            def projected(a, g, q):
                at(dve, s_proj_pe, TILES, a, q + 1)
                at(dve, s_turned_done, TILES, a, q - 1)
                at(dve, s_v_new_done, TILES, a, q - 1)
                nc.vector.tensor_tensor(proj[:, q % 2, :], ring[1][:, 0:PW], of_group(bias, g, PW), ALU.add) \
                    .then_inc(s_proj_done, 1)

            def maximum(b, q, h):
                if h == 0:
                    at(dve, s_neg_done, TILES, b, q)
                at(dve, s_max_pe, TILES * GROUP, b, GROUP * q + h + 1)
                k0 = max(q - 1, 0)
                cols = (min(q + 1, TILES - 1) - k0 + 1) * P
                m0 = (k0 - q + 1) * P
                stand_apart(dve, s_dve_passed)
                nc.vector.tensor_tensor_reduce(junk[:, h % 2, 0:cols], ring[h % 2][:, 0:cols], mask[:, m0:m0 + cols],
                                               1.0, LOWEST, ALU.add, ALU.max, row_max[:, h:h + 1]) \
                    .then_inc(s_max_done, 1)

            def negated(b, g, q):
                at(dve, s_max_done, TILES * GROUP, b, GROUP * (q + 1))
                at(dve, s_sink_done, TILES, b, q + 1)
                n_s = of_group(neg_sink, g, GROUP)
                nc.vector.scalar_tensor_tensor(neg_max[:, :], row_max[:, :], -1.0, n_s, ALU.mult, ALU.min) \
                    .then_inc(s_small_self, 1)
                at(dve, s_small_self, TILES, b, q + 1)
                parts = neg_parts[:, q, :].rearrange("p (h w) -> p h w", w=2)
                nc.vector.tensor_copy(parts[:, :, 0], neg_max[:, :]).then_inc(s_mh_done, 1)
                nc.vector.tensor_tensor(sink_arg[:, q, :], neg_max[:, :], n_s, ALU.subtract)
                at(dve, s_mh_done, TILES, b, q + 1)
                nc.vector.tensor_tensor(parts[:, :, 1], neg_max[:, :], parts[:, :, 0].bitcast(F32),
                                        ALU.subtract).then_inc(s_neg_done, 1)

            def normalised(c, q, par):
                at(dve, s_sink_done, TILES, c + 1, q + 1)
                at(dve, s_pv_pe, TILES, c + 1, q + 1)
                nc.vector.tensor_tensor(den[:, :], pv[:, :, D], sink_exp[:, par, q, :], ALU.add) \
                    .then_inc(s_norm_self, 1)
                at(dve, s_norm_self, 2 * TILES, c + 1, 2 * q + 1)
                nc.vector.reciprocal(rden[:, :], den[:, :]).then_inc(s_norm_self, 1)
                at(dve, s_norm_self, 2 * TILES, c + 1, 2 * q + 2)
                nc.vector.tensor_tensor(o_norm[:, :, :], pv[:, :, 0:D],
                                        rden[:, :].rearrange("p (h a) -> p h a", a=1).broadcast_to([P, GROUP, D]),
                                        ALU.mult).then_inc(s_norm_done, 1)

            def o_low(c, q):
                at(dve, s_oT_hi_done, TILES, c + 1, q + 1)
                nc.vector.tensor_tensor(oT_lo[:, q % 2, :], ring[2][:, 0:KT * P], oT_hi[:, q % 2, :].bitcast(F32),
                                        ALU.subtract).then_inc(s_oT_lo_done, 1)

            def largest():
                dve.wait_ge(s_ln_done, BATCH)
                nc.vector.tensor_reduce(amax[:, :], absmax[:, :], AX.X, ALU.max).then_inc(s_amax_done, 1)
                dve.wait_ge(s_amax_pe, 1)
                nc.vector.tensor_reduce(scale_row[:, 0:1], ring[0][0:1, 0:P], AX.X, ALU.max).then_inc(s_amax_self, 1)
                dve.wait_ge(s_amax_self, 1)
                nc.vector.tensor_scalar(scale_row[:, 1:2], scale_row[:, 0:1], 1.0 / FP8_MAX, SCALE_EPS, ALU.mult,
                                        ALU.max).then_inc(s_amax_self, 1)
                dve.wait_ge(s_amax_self, 2)
                nc.vector.reciprocal(scale_row[:, 2:3], scale_row[:, 1:2]).then_inc(s_amax_self, 1)
                dve.wait_ge(s_scale_pe, 1)
                nc.vector.tensor_copy(inv_scale[:, :], ring[1][:, 0:1]).then_inc(s_inv_ready, 1)

            def beside(n, k, q, half):
                fill = filling(k, q)
                if fill is not None:
                    m = fill + 2
                    if m <= BATCH:
                        buf, got = (x_in, s_x_got) if m % 2 == 0 else (gate, s_x_odd_got)
                        dve.wait_ge(got, 16 * (m // 2 + 1))
                        statistics(m, buf, range(TILES))
                        moments_of(m)
                        if m > 2:
                            measure(m - 1)
                    else:
                        largest()
                elif (k, q) == (0, 0):
                    dve.wait_ge(s_x_got, n * 16 + 16 * (BATCH // 2 + 2))
                    statistics(n + (BATCH + 1), x_in, (0, 1))
                elif (k, q) == (0, 1):
                    gated(n, 0)
                elif (k, q) == (0, 2):
                    statistics(n + (BATCH + 1), x_in, (2, 3))
                    moments_of(n + (BATCH + 1))
                elif (k, q) == (0, 3):
                    gated(n, 1)
                elif (k, q) == (1, 0):
                    normalise(n + (BATCH + 1), x_in, (0, 1))
                elif (k, q) == (1, 1):
                    normalise(n + (BATCH + 1), x_in, (2, 3))
                elif (k, q) == (1, 2):
                    ffn_bias_on(n, 0)
                elif (k, q) == (1, 3):
                    ffn_bias_on(n, 1)
                elif (k, q) == (KV - 2, 0):
                    x_low(n + 1, 0)
                    x_low(n + 1, 1)
                elif (k, q) == (2, 0):
                    ffn_clamp(n, half)
                elif (k, q) == (2, 2):
                    ffn_one_more(n, half)
                elif k in (2, 3) and 3 <= (k - 2) * TILES + q <= 6:
                    ffn_invert(n, half, (k - 2) * TILES + q - 3)
                elif (k, q) == (3, 3):
                    ffn_gate(n, half)
                elif (k, q) in ((KV - 2, 2), (KV - 1, 0)):
                    exponents(n + 1, k - (KV - 2))
                elif (k, q) in ((KV - 2, 3), (KV - 1, 1)):
                    quantise(n + 1, k - (KV - 2))

            def step(it, par, groups, n=None, k=None, half=None):
                a, b, c, _ = groups
                for q in range(TILES):
                    b_group = b if q >= 1 else c
                    beside(n, k, q, half)
                    projected(it + 2, a, q)
                    b_step, b_tile = back(it + 1, q, 1)
                    for h in range(GROUP):
                        if c is not None and h == GROUP - 1 and q != 1:
                            o_low(*back(it, q, 2))
                        if b_group is not None:
                            maximum(b_step, b_tile, h)
                    if b_group is not None:
                        negated(b_step, b_group, b_tile)
                    if c is not None and q == 1:
                        o_low(*back(it, q, 2))
                    if c is not None:
                        normalised(*back(it, q, 1), par if q >= 1 else 1 - par)
                    fill = filling(k, q)
                    if fill is not None and fill + 2 <= BATCH:
                        dve.wait_ge(s_ln_done, fill + 2)
                        normalise(fill + 2, x_in if fill % 2 == 0 else gate, range(TILES))
                    if fill is not None and W_CHUNKS + fill < N_CHUNKS:
                        chunk_low(W_CHUNKS + fill)

            nc.vector.memset(kT_low[D:D + 32, :, :].bitcast(F32), 1.0).then_inc(s_ones_ready, 1)
            dve.sem_inc(s_norm_self, 2 * (TILES - 1))
            dve.sem_inc(s_gate_done, 2)
            dve.wait_ge(s_x_got, 16)
            statistics(0, x_in, range(TILES))
            moments_of(0)
            normalise(0, x_in, range(TILES))
            measure(0)
            chunk_low(0)
            x_low(0, 0)
            x_low(0, 1)
            chunk_low(1)
            dve.wait_ge(s_x_odd_got, 16)
            statistics(1, gate, range(TILES))
            moments_of(1)
            chunk_low(2)
            normalise(1, gate, range(TILES))
            chunk_low(3)
            measure(1)
            dve.wait_ge(s_const_in, 16 * len(consts))
            nc.vector.tensor_scalar(neg_sink[:, :], neg_sink[:, :], -1.0, None, ALU.mult).then_inc(s_sink_negated, 1)
            dve.wait_ge(s_sink_negated, 1)

            def first():
                for j in range(2):
                    exponents(0, j)
                    quantise(0, j)
                dve.wait_ge(s_bias_in, 16)

            run_steps(dve, step, first)
            o_low(*back(BATCH * KV, 0, 2))
            normalised(BATCH * KV - 1, TILES - 1, (BATCH * KV - 1) % 2)
            gated(BATCH, 0)
            o_low(*back(BATCH * KV, 1, 2))
            gated(BATCH, 1)

        @block.tensor
        def _(pe):
            def ring2_read(it, q):
                at(pe, s_oT_lo_done, TILES, it + 1, q - 2)

            def turn_x(n, k):
                for t in range(TILES):
                    last = nc.tensor.transpose(ring[2 - k][:, t * P:(t + 1) * P], xn[:, t, k * P:(k + 1) * P],
                                               ident[:, :])
                last.then_inc(s_xT_pe, 1)

            def turn_xq(n, k):
                for t in range(TILES):
                    last = nc.tensor.matmul(ring[2][:, t * P:(t + 1) * P], xq[:, t, k * P:(k + 1) * P],
                                            ident_b[:, :], start=True, stop=True)
                last.then_inc(s_xqT_pe, 1)

            def ffn(b, j):
                pe.wait_ge(s_xqT_done, b * KT + KT)
                for t in range(2):
                    tile = 2 * j + t
                    for k in range(KT):
                        for part in (ffn_hi, ffn_lo):
                            last = nc.tensor.matmul(ring[2][:, t * M:(t + 1) * M], xqT[:, k, tile * P:(tile + 1) * P],
                                                    part[:, k * M:(k + 1) * M], start=(k == 0 and part is ffn_hi),
                                                    stop=(k == KT - 1 and part is ffn_lo))
                last.then_inc(s_ffn_pe, 1)

            def project(a, g, q):
                products = [(left, right, k) for k in range(KT)
                            for left, right in ((xT_hi, w_hi), (xT_hi, w_lo), (xT_lo, w_hi))]
                for n, (left, right, k) in enumerate(products):
                    last = nc.tensor.matmul(ring[1][:, 0:PW], left[:, k, q * P:(q + 1) * P],
                                            of_group(right[:, k, :], g, PW), start=(n == 0),
                                            stop=(n == len(products) - 1))
                last.then_inc(s_proj_pe, 1)

            def turn_q_full(b, q, par):
                at(pe, s_lo_done, TILES, b, q + 1)
                at(pe, s_max_done, TILES * GROUP, b, GROUP * q - 1)
                for h in range(GROUP):
                    last = nc.tensor.matmul(ring[0][:, h * P:(h + 1) * P], qk_parts[:, par, q, h * HW:h * HW + 2 * D],
                                            ident_r[:, :], start=True, stop=True)
                last.then_inc(s_qfull_pe, 1)

            def turn_k(b, par, low):
                at(pe, s_lo_done, TILES, b, TILES)
                k0 = GROUP * HW
                if low:
                    at(pe, s_kT_done, 2, b, 1)
                for t in range(TILES):
                    src = qk_parts[:, par, t, k0:k0 + D] if low else qk_parts[:, par, t, k0 + D:k0 + 3 * D]
                    last = nc.tensor.matmul(ring[2][0:(D if low else 2 * D), t * P:(t + 1) * P], src,
                                            ident_r[:, :], start=True, stop=True)
                last.then_inc(s_kT_pe, 1)

            def turn_max(b, q):
                at(pe, s_neg_done, TILES, b, q + 1)
                nc.tensor.matmul(ring[2][0:NR, 0:P], neg_parts[:, q, :], ident_r[:, :], start=True, stop=True) \
                    .then_inc(s_max_turned_pe, 1)

            def score_rows(b, q, h, par, it, now):
                if h == 0:
                    at(pe, s_qfull_done, TILES, b, q + 1)
                elif h == 1:
                    at(pe, s_proj_done, TILES, it + 2, now + 1)
                else:
                    at(pe, s_max_done, TILES * GROUP, b, GROUP * q + h - 1)
                if q == 0 and h == 0:
                    at(pe, s_kT_done, 2, b, 1)
                k0 = max(q - 1, 0)
                cols = (min(q + 1, TILES - 1) - k0 + 1) * P
                nc.tensor.matmul(ring[h % 2][:, 0:cols], qT_full[:, q, h * P:(h + 1) * P],
                                 kT_high[:, par, k0 * P:k0 * P + cols], start=True, stop=True).then_inc(s_max_pe, 1)

            def scores(c, q, n, par):
                k, blk = BLOCKS[q][n], FIRST[q] + n
                if n == 0:
                    at(pe, s_qhigh_done, TILES, c, q + 1)
                    at(pe, s_max_rows_done, TILES, c, q + 1)
                    if q == 0:
                        at(pe, s_kT_done, 2, c, 2)
                at(pe, s_exp_done, NB, c + 1, blk - 1)
                nc.tensor.matmul(score[blk % 2][:, :], kT_high[:, par, k * P:(k + 1) * P], qT_full[:, q, :],
                                 start=True, stop=False)
                nc.tensor.matmul(score[blk % 2][:, :], kT_low[0:D + NR, par, k * P:(k + 1) * P],
                                 qT_high[0:D + NR, q, :], start=False, stop=True).then_inc(s_score_pe, 1)

            def weigh(c, q, h, par):
                if h == 0:
                    if q == 0:
                        at(pe, s_v_ready, 1, c, 1)
                    at(pe, s_exp_done, NB, c + 1, FIRST[q + 1])
                    at(pe, s_cut_done, NCUT, c + 1, CUT[q + 1])
                    at(pe, s_norm_done, TILES, c + 1, q)
                for n, k in enumerate(BLOCKS[q]):
                    last = nc.tensor.matmul(pv[:, h, :], prob[:, q % 2 * 3 + n, h * P:(h + 1) * P],
                                            v[:, par, k, :], start=(n == 0), stop=(n == len(BLOCKS[q]) - 1))
                if h == GROUP - 1:
                    last.then_inc(s_pv_pe, 1)

            def turn_o(c, q):
                at(pe, s_norm_done, TILES, c + 1, q + 1)
                o_flat = o_norm[:, :, :].rearrange("p h d -> p (h d)")
                for k in range(KT):
                    last = nc.tensor.transpose(ring[2][:, k * P:(k + 1) * P], o_flat[:, k * P:(k + 1) * P],
                                               ident[:, :])
                last.then_inc(s_oT_pe, 1)

            def out_project(c, g, q, fresh=False):
                at(pe, s_oT_lo_done, TILES, c + 1, q + 1)
                for k in range(KT):
                    for left, right in ((oT_hi, wo_hi), (oT_hi, wo_lo), (oT_lo, wo_hi)):
                        w_g = right[:, (g * KT + k) * M:(g * KT + k + 1) * M] if isinstance(g, int) else \
                            right[:, bass.ds(g * (KT * M) + k * M, M)]
                        last = nc.tensor.matmul(acc[q // 2][:, (q % 2) * M:(q % 2 + 1) * M],
                                                left[:, q % 2, k * P:(k + 1) * P], w_g,
                                                start=fresh and k == 0 and left is oT_hi and right is wo_hi, stop=True,
                                                skip_group_check=True)
                last.then_inc(s_wo_pe, 1)

            def largest():
                pe.wait_ge(s_amax_done, 1)
                pe.wait_ge(s_max_done, TILES * GROUP - 2 * GROUP)
                nc.tensor.transpose(ring[0][0:1, 0:P], amax[:, :], ident[:, :]).then_inc(s_amax_pe, 1)
                pe.wait_ge(s_amax_self, 3)
                nc.tensor.matmul(ring[1][:, 0:1], ones[:, :], scale_row[:, 2:3], start=True, stop=True) \
                    .then_inc(s_scale_pe, 1)

            def beside(n, k, q):
                if filling(k, q) == BATCH - 1:
                    largest()
                elif k == 1 and q >= 2:
                    ring2_read(n * KV + k, q)
                    ffn(n, q - 2)
                elif (k, q) == (KV - 2, 0):
                    pe.wait_ge(s_xn_done, n + (BATCH + 2))
                    ring2_read(n * KV + k, q)
                    turn_x(n + 1, 0)
                    at(pe, s_max_done, TILES * GROUP, n * KV + k, TILES * GROUP - GROUP)
                    turn_x(n + 1, 1)
                elif k == KV - 1 and q >= 2:
                    pe.wait_ge(s_xq_done, n * 2 + 4)
                    ring2_read(n * KV + k, q)
                    turn_xq(n + 1, q - 2)

            def step(it, par, groups, n=None, k=None, half=None):
                a, b, c, before = groups
                with_c = c is not None
                for q in range(TILES):
                    with_b1 = (b if q >= 1 else c) is not None
                    with_b2 = (b if q >= 2 else c) is not None
                    b1, b1_par = back(it + 1, q, 1), 1 - par if q >= 1 else par
                    b2 = back(it + 1, q, 2)
                    c1, c1_par = back(it, q, 1), par if q >= 1 else 1 - par
                    new_x = (k, q) == (KV - 2, 0)

                    def projection():
                        if new_x:
                            pe.wait_ge(s_xT_lo_done, n * KT + 2 * KT)
                        at(pe, s_max_done, TILES * GROUP, it + 1, GROUP * (q - 1))
                        project(it + 2, a, q)

                    if with_c:
                        scores(it, q, 0, par)
                    if q == 1 and b is not None:
                        ring2_read(it, q)
                        turn_k(it + 1, 1 - par, False)
                    if with_c:
                        scores(it, q, 1, par)
                    if not new_x:
                        beside(n, k, q)
                    if filling(k, q) == BATCH - 1:
                        pe.wait_ge(s_inv_ready, 1)
                    if with_b1:
                        turn_q_full(*b1, b1_par)
                    if new_x:
                        beside(n, k, q)
                    if not with_c:
                        at(pe, s_proj_done, TILES, it + 2, q)
                    if not new_x:
                        projection()
                    if q == 1 and b is not None:
                        turn_k(it + 1, 1 - par, True)
                    if with_c and len(BLOCKS[q]) > 2:
                        scores(it, q, 2, par)

                    def maxima_turn():
                        if new_x:
                            pe.wait_ge(s_xT_lo_done, n * KT + (KT + 1))
                        elif k == 1 and q >= 2:
                            pe.wait_ge(s_ffn_z, n * 2 + (q - 1))
                        elif k == KV - 1 and q >= 2:
                            pe.wait_ge(s_xqT_done, n * KT + (KT + q - 1))
                        elif q == 1:
                            at(pe, s_kT_done, 2, it + 1, 2)
                        else:
                            ring2_read(it, q)
                            if not with_c or q == 0:
                                at(pe, s_max_rows_done, TILES, it + 1, q - 2)
                        if with_b2:
                            turn_max(*b2)

                    def row(h):
                        if with_b1:
                            score_rows(*b1, h, b1_par, it, q)

                    def weighed(h):
                        if with_c:
                            weigh(*c1, h, c1_par)

                    def heads_turn():
                        if with_c:
                            at(pe, s_max_rows_done, TILES, it + 1, q - 1)
                            turn_o(*back(it, q, 2))

                    def outwards():
                        if with_c:
                            c3, c3_tile = back(it, q, 3)
                            fresh = (k, q) in ((0, 3), (1, 1))
                            if (k, q) in ((0, 3), (1, 1)):
                                pe.wait_ge(s_fin_read, n * 2 + 1 + k)
                            out_project(c3, c if q == 3 else before, c3_tile, fresh)

                    if new_x:
                        row(0)
                        weighed(0)
                        weighed(1)
                        maxima_turn()
                        projection()
                        weighed(2)
                        weighed(3)
                        row(1)
                        heads_turn()
                        row(2)
                        outwards()
                        row(3)
                    elif q == 0:
                        maxima_turn()
                        row(0)
                        weighed(0)
                        weighed(1)
                        row(1)
                        weighed(2)
                        row(2)
                        heads_turn()
                        weighed(3)
                        row(3)
                        outwards()
                    elif q == 1:
                        row(0)
                        weighed(0)
                        weighed(1)
                        maxima_turn()
                        row(1)
                        weighed(2)
                        row(2)
                        weighed(3)
                        row(3)
                        outwards()
                        heads_turn()
                    else:
                        maxima_turn()
                        row(0)
                        weighed(0)
                        row(1)
                        weighed(1)
                        heads_turn()
                        row(2)
                        weighed(2)
                        row(3)
                        weighed(3)
                        outwards()

            pe.wait_ge(s_id_ready, 6)
            pe.wait_ge(s_ones_ready, 2)
            pe.wait_ge(s_xn_done, 1)
            turn_x(0, 0)
            turn_x(0, 1)
            pe.wait_ge(s_const_in, 16 * len(consts))
            for j in range(2):
                nc.tensor.matmul(acc[j][:, :], ones[:, :], bias[0:1, 0:2 * M], start=True, stop=True,
                                 skip_group_check=True)
            pe.wait_ge(s_xT_lo_done, KT)
            pe.wait_ge(s_w_lo_done, W_CHUNKS)
            pe.sem_inc(s_pv_pe, TILES - 1)
            pe.sem_inc(s_oT_pe, TILES - 2)
            pe.sem_inc(s_wo_pe, TILES - 3)

            def first():
                pe.wait_ge(s_xq_done, 2)
                pe.wait_ge(s_max_rows_done, 2)
                turn_xq(0, 0)
                pe.wait_ge(s_xqT_done, 1)
                turn_xq(0, 1)
                pe.wait_ge(s_xqT_done, KT)
                pe.wait_ge(s_w_lo_done, N_CHUNKS)

            run_steps(pe, step, first)
            END = BATCH * KV
            for h in range(GROUP):
                weigh(END - 1, TILES - 1, h, (END - 1) % 2)
            ring2_read(END, 0)
            turn_o(END - 1, TILES - 2)
            out_project(END - 1, KV - 1, TILES - 3)
            ring2_read(END, 1)
            turn_o(END - 1, TILES - 1)
            out_project(END - 1, KV - 1, TILES - 2)
            out_project(END - 1, KV - 1, TILES - 1)


def kernel(L0_attn_hidden_states, L0_attn_Wq, L0_attn_bq, L0_attn_Wk, L0_attn_bk, L0_attn_Wv, L0_attn_bv, L0_attn_Wo,
           L0_attn_bo, L0_attn_sinks, L0_ffn_weight, L0_ffn_weight_scale, L0_ffn_bias):
    import concourse.bacc as bacc
    from concourse.bass_utils import run_bass_kernel_spmd

    def host(a):
        return np.asarray(a)

    wq = host(L0_attn_Wq).reshape(KT, P, KV, QW)
    wk = host(L0_attn_Wk).reshape(KT, P, KV, D)
    wv = host(L0_attn_Wv).reshape(KT, P, KV, D)
    w_qkv = np.concatenate([wq, wk, wv], axis=3).reshape(KT, P, KV * PW)
    b_qkv = np.concatenate([host(L0_attn_bq).reshape(KV, QW), host(L0_attn_bk), host(L0_attn_bv)], axis=1).reshape(-1)
    w_o = host(L0_attn_Wo).reshape(KV * KT, P, M).transpose(1, 0, 2).reshape(P, KV * KT * M)
    w_ffn = host(L0_ffn_weight).T.reshape(KT, P, M).transpose(1, 0, 2).reshape(P, KT * M)

    inv_freq = np.float32(1.0) / np.float32(WAVELENGTH) ** (np.arange(D // 2, dtype=np.float32) * np.float32(2.0) / D)
    freqs = np.arange(SEQ, dtype=np.float32)[:, None] * inv_freq.astype(np.float32)[None, :]
    c, sn = np.cos(freqs) * np.float32(SCALE), np.sin(freqs) * np.float32(SCALE)
    cos = np.repeat(c, 2, axis=1).reshape(TILES, P, D).transpose(1, 0, 2)
    sin = np.stack([-sn, sn], axis=-1).reshape(TILES, P, D).transpose(1, 0, 2)

    arrays = {"x": host(L0_attn_hidden_states), "w_qkv": w_qkv, "b_qkv": b_qkv, "w_o": w_o, "b_o": host(L0_attn_bo),
              "sinks": host(L0_attn_sinks), "w_ffn": w_ffn, "w_scale": host(L0_ffn_weight_scale).reshape(1),
              "b_ffn": host(L0_ffn_bias), "rope_cos": cos.astype(np.float32), "rope_sin": sin.astype(np.float32)}
    arrays = {f"in_{n}": np.ascontiguousarray(a) for n, a in arrays.items()}
    nc = bacc.Bacc("TRN2", target_bir_lowering=False, num_devices=1)
    args = [nc.dram_tensor(n, a.shape, mybir.dt.from_np(a.dtype), kind="ExternalInput").ap()
            for n, a in arrays.items()]
    out = nc.dram_tensor("out", (BATCH, SEQ, M), F32, kind="ExternalOutput").ap()
    gated_window_attention(nc, *args, out)
    result = run_bass_kernel_spmd(nc, [arrays], core_ids=[0])
    return result.results[0]["out"]
```
